# Optimizing a Trainium2 kernel written in Bass

```python
import numpy as np
import jax
import jax.numpy as jnp

def _softmax(x, axis=-1):
    return jax.nn.softmax(x, axis=axis)

def _gelu(x):
    return jax.nn.gelu(x, approximate=True)

def _silu(x):
    return jax.nn.silu(x)

def _sigmoid(x):
    return jax.nn.sigmoid(x)

def _layernorm(x, axis=-1, eps=1e-05):
    m = jnp.mean(x, axis=axis, keepdims=True)
    v = jnp.var(x, axis=axis, keepdims=True)
    return (x - m) / jnp.sqrt(v + eps)

def _scatter_add(tgt, idx, src, axis=0):
    return tgt.at[idx].add(src)

def _segment_sum(src, seg, n):
    return jax.ops.segment_sum(src, seg, n)
kernel_name = 'mk_adaln_ffn_d1_seqx_r4_96a314'

def setup_inputs(seed: int=0):
    np.random.seed(seed)
    _w = jnp.asarray

    def _rec_inputs():
        import jax
        import jax.numpy as jnp
        _rk = jax.random.key(seed)
        x = -7.109e-05 + 0.9999 * jax.random.normal(jax.random.fold_in(_rk, 1), (32, 64, 512), jnp.float32)
        _lenS = 64 - jax.random.randint(jax.random.fold_in(_rk, 7), (32,), 0, max(1, 64 // 4) + 1, jnp.int32)
        _lenS2 = 64 - jax.random.randint(jax.random.fold_in(_rk, 8), (32,), 0, max(1, 64 // 4) + 1, jnp.int32)
        itok_B_1_198 = jax.random.randint(jax.random.fold_in(_rk, 11), (32,), 1, 199, jnp.int32)
        return (x, itok_B_1_198)
    x, itok_B_1_198 = _rec_inputs()

    def _L0_cond_setup():
        import jax, jax.numpy as jnp
        import numpy as np
        B, C, T = (128, 64, 512)
        S, D = (200, 64)
        key = jax.random.key(seed)
        k1, k2, k3 = jax.random.split(key, 3)
        x = jax.random.normal(k1, (B, C, T), dtype=jnp.float32)
        conditions = jax.random.randint(k2, (B,), 0, S, dtype=jnp.int64)
        weights = jax.random.normal(k3, (S, C, D), dtype=jnp.float32) / jnp.sqrt(jnp.float32(C))
        return {'x': x, 'conditions': conditions, 'weights': weights}
    _L0_cond_all = _L0_cond_setup()
    _L0_cond_in = {k: v for k, v in _L0_cond_all.items() if k in ('weights',)}
    del _L0_cond_all

    def _L0_ffn_setup():
        import jax, jax.numpy as jnp
        import numpy as np
        NUM_EXPERTS = 8
        TOP_K = 2
        key = jax.random.key(seed)
        ks = jax.random.split(key, 7)
        B, S, H, I, E = (4, 512, 512, 512, NUM_EXPERTS)
        sc = 0.02
        return {'hidden_states': jax.random.normal(ks[0], (B, S, H), dtype=jnp.float32), 'gate_w': jax.random.normal(ks[1], (E, H), dtype=jnp.float32) * sc, 'gate_b': jax.random.normal(ks[2], (E,), dtype=jnp.float32) * sc, 'w1': jax.random.normal(ks[3], (E, 2 * I, H), dtype=jnp.float32) * sc, 'b1': jax.random.normal(ks[4], (E, 2 * I), dtype=jnp.float32) * sc, 'w2': jax.random.normal(ks[5], (E, H, I), dtype=jnp.float32) * sc, 'b2': jax.random.normal(ks[6], (E, H), dtype=jnp.float32) * sc}
    _L0_ffn_all = _L0_ffn_setup()
    _L0_ffn_in = {k: v for k, v in _L0_ffn_all.items() if k in ('gate_w', 'gate_b', 'w1', 'b1', 'w2', 'b2')}
    del _L0_ffn_all
    return {'x': x, 'itok_B_1_198': itok_B_1_198, 'L0_cond_weights': _L0_cond_in['weights'], 'L0_ffn_gate_w': _L0_ffn_in['gate_w'], 'L0_ffn_gate_b': _L0_ffn_in['gate_b'], 'L0_ffn_w1': _L0_ffn_in['w1'], 'L0_ffn_b1': _L0_ffn_in['b1'], 'L0_ffn_w2': _L0_ffn_in['w2'], 'L0_ffn_b2': _L0_ffn_in['b2']}

def reference(x, itok_B_1_198, L0_cond_weights, L0_ffn_gate_w, L0_ffn_gate_b, L0_ffn_w1, L0_ffn_b1, L0_ffn_w2, L0_ffn_b2):
    import jax
    import jax.numpy as jnp

    def _L0_cond_ref(x, conditions, weights):
        import jax, jax.numpy as jnp
        import numpy as np
        B, C, T = (128, 64, 512)
        S, D = (200, 64)
        w = weights[conditions]
        return jnp.einsum('bct,bcd->bdt', x, w)

    def _L0_ffn_ref(hidden_states, gate_w, gate_b, w1, b1, w2, b2):
        import jax, jax.numpy as jnp
        import numpy as np
        NUM_EXPERTS = 8
        TOP_K = 2
        B, S, H = hidden_states.shape
        x = hidden_states.reshape(-1, H)
        logits = x @ gate_w.T + gate_b
        top_vals, top_idx = jax.lax.top_k(logits, TOP_K)
        routing = jax.nn.softmax(top_vals.astype(jnp.float32), axis=-1).astype(x.dtype)
        out = jnp.zeros_like(x)
        E = w1.shape[0]
        for e in range(E):
            h = x @ w1[e].T + b1[e]
            x_glu = h[:, 0::2]
            x_lin = h[:, 1::2]
            y = x_glu * jax.nn.sigmoid(1.702 * x_glu) * (x_lin + 1.0)
            ye = y @ w2[e].T + b2[e]
            we = jnp.sum(routing * (top_idx == e), axis=-1)
            out = out + ye * we[:, None]
        return out.reshape(B, S, H)
    x = x + _L0_ffn_ref(_L0_cond_ref(x, itok_B_1_198, L0_cond_weights), L0_ffn_gate_w, L0_ffn_gate_b, L0_ffn_w1, L0_ffn_b1, L0_ffn_w2, L0_ffn_b2)
    return x

_drawn_inputs = setup_inputs


def setup_inputs(seed=0):
    import zlib

    import numpy as np

    out = dict(_drawn_inputs(seed))
    spreads = {}
    factors = {'L0_ffn_gate_b': 3.649, 'L0_ffn_b1': 8.0, 'L0_ffn_b2': 3.97}
    for name, (base, spread) in spreads.items():
        noise = np.random.default_rng([zlib.crc32(name.encode()), seed]).standard_normal(out[name].shape)
        drawn = base * np.exp(spread * noise) if base else spread * noise
        out[name] = jnp.asarray(drawn.astype(out[name].dtype))
    for name, factor in factors.items():
        out[name] = (out[name] * factor).astype(out[name].dtype)
    return out
```

```python
from contextlib import ExitStack

import concourse.bass as bass
from concourse import mybir

P = 128
ALU = mybir.AluOpType
ACT = mybir.ActivationFunctionType
F32 = mybir.dt.float32
BF16 = mybir.dt.bfloat16
I32 = mybir.dt.int32
AX_X = mybir.AxisListType.X

RING = 3
FLOOR = -3.0e38


def adaln_moe_kernel(nc, x, cond, cond_w, gate_w, gate_b, ffn_w, ffn_b, x0_rows, out):
    TOKENS, H = x.shape
    B = cond.shape[1]
    C = TOKENS // B
    E = ffn_w.shape[0]
    K = H // P
    I = H
    NT = TOKENS // P
    SLOTS = (2 * TOKENS + E * (P - 1)) // P
    NB = SLOTS + 1
    NP = 2 * NT
    GLU, LIN, DOWN = 0, K * I, 2 * K * I
    WLEN = 2 * K * I + K * H
    BG, BL, BD = 0, I, 2 * I
    BLEN = 2 * I + H
    NX = 4
    TX = NT // NX
    assert B == 2 * NT and C == 64 and ffn_w.shape[2] == WLEN and ffn_b.shape[1] == BLEN

    with ExitStack() as ctx:
        def sb(name, shape, dt=F32):
            return ctx.enter_context(nc.sbuf_tensor(name, shape, dt))

        def psum(name, shape):
            return ctx.enter_context(nc.psum_tensor(name, shape, F32))

        def sem(name):
            return ctx.enter_context(nc.semaphore(name))

        ident = sb("ident", [P, P])
        before = sb("before", [P, P], BF16)
        ones = sb("ones", [P, P], BF16)
        row_id = sb("row_id", [P, P])
        token_id = sb("token_id", [P, NP])
        bounds = sb("bounds", [P, NB])
        slot_id = sb("slot_id", [P, SLOTS])
        expert_id = sb("expert_id", [P, E])
        rev_id = sb("rev_id", [P, E])
        fill_id = sb("fill_id", [P, NT])
        earlier = sb("earlier", [P, E, E])
        pad_id = sb("pad_id", [P, 1])
        neg_pad = sb("neg_pad", [P, 1])
        cond_sb = sb("cond_sb", [1, B], I32)
        x_sb = sb("x_sb", [P, NT, H])
        w_diag = sb("w_diag", [P, NT, P])
        x0_sb = sb("x0_sb", [P, NT, H])
        x0T = sb("x0T", [P, 2, K * P])
        gw = sb("gw", [P, K, E])
        gb = sb("gb", [P, E])
        logits = sb("logits", [P, NT, E])
        rest = sb("rest", [P, NT, E])
        hit = sb("hit", [P, NT, E])
        key = sb("key", [P, NT, E])
        best = sb("best", [P, 2, NT])
        pick = sb("pick", [P, 2, NT])
        chosen = sb("chosen", [P, 2, NT, E])
        gap = sb("gap", [P, NT])
        egap = sb("egap", [P, NT])
        den = sb("den", [P, NT])
        share = sb("share", [P, 2, NT])
        mask = sb("mask", [P, NT + 1, E], BF16)
        full = sb("full", [P, E, NT])
        tiles_of = sb("tiles_of", [P, E])
        bef = sb("bef", [P, E, E])
        base = sb("base", [P, E])
        base_rows = sb("base_rows", [P, E])
        place_e = sb("place_e", [P, NT, E])
        place_k = sb("place_k", [P, 2, NT, E])
        place = sb("place", [P, NP])
        past = sb("past", [P, NP, NB])
        count = sb("count", [P, NP])
        row_of = sb("row_of", [P, NP])
        spare = x0_sb[:].rearrange("p n h -> p (n h)")
        row_hot = spare[:, 0:NP * P].rearrange("p (j r) -> p j r", r=P)
        slot_hot = spare[:, NP * P:NP * (P + 3 * SLOTS)].rearrange("p (j a s) -> p j a s", a=3, s=SLOTS)
        table = sb("table", [P, 3, SLOTS])
        fill = sb("fill", [P, SLOTS])
        tokens = sb("tokens", [P, SLOTS], I32)
        used = sb("used", [1, E])
        begun = sb("begun", [1, SLOTS, E])
        begun_id = sb("begun_id", [1, SLOTS, E])
        order = sb("order", [1, SLOTS + 1])
        expert_of = sb("expert_of", [1, SLOTS])
        m = sb("m", [1, 8, SLOTS])
        meta = sb("meta", [1, SLOTS + 1, 4], I32)
        W = sb("W", [P, RING * WLEN])
        BI = sb("BI", [P, RING * BLEN])
        xg = sb("xg", [P, H])
        xT = sb("xT", [P, K, P])
        g = sb("g", [P, I])
        lin = sb("lin", [P, I])
        sig = sb("sig", [P, I])
        gs = sb("gs", [P, I])
        y = sb("y", [P, I])
        yT = sb("yT", [P, K, P])
        zb = sb("zb", [P, H])
        zw = sb("zw", [P, H])
        gather_at = sb("gather_at", [P, 1], I32)
        scatter_at = sb("scatter_at", [P, 1], I32)

        ps_glu = psum("ps_glu", [P, I])
        ps_lin = psum("ps_lin", [P, I])
        ps_z = psum("ps_z", [P, H])
        ps_xT = psum("ps_xT", [P, K * P])
        ps_yT = psum("ps_yT", [P, K * P])
        ps_log = psum("ps_log", [P, NT * E])
        ps_rank = psum("ps_rank", [P, (NT + 1) * E])
        ps_tab = psum("ps_tab", [P, 3 * SLOTS])
        ps_x0 = [ps_glu, ps_lin]
        ps_x0T = [ps_xT, ps_yT]

        s_cond = sem("s_cond")
        s_gate = sem("s_gate")
        s_x = [sem(f"s_x_part{n}") for n in range(NX)]
        s_wz = sem("s_wz")
        s_wd = sem("s_wd")
        s_const = sem("s_const")
        s_x0 = sem("s_x0")
        s_x0c = sem("s_x0c")
        s_x0T = sem("s_x0T")
        s_x0Tc = sem("s_x0Tc")
        s_log = sem("s_log")
        s_rows = sem("s_rows")
        s_init = sem("s_init")
        s_first = sem("s_first")
        s_gap = sem("s_gap")
        s_egap = sem("s_egap")
        s_mask = sem("s_mask")
        s_rank = sem("s_rank")
        s_hot = sem("s_hot")
        s_tab = sem("s_tab")
        s_route = sem("s_route")
        s_meta = sem("s_meta")
        s_dve = sem("s_dve")
        s_pool = sem("s_pool")
        loaded = sem("loaded")
        gathered = sem("gathered")
        xT_made = sem("xT_made")
        xT_ready = sem("xT_ready")
        glu_made = sem("glu_made")
        lin_made = sem("lin_made")
        g_ready = sem("g_ready")
        sig_ready = sem("sig_ready")
        part_ready = sem("part_ready")
        y_ready = sem("y_ready")
        yT_made = sem("yT_made")
        yT_ready = sem("yT_ready")
        z_made = sem("z_made")
        zb_ready = sem("zb_ready")
        zw_ready = sem("zw_ready")
        scattered = sem("scattered")
        at_ready = sem("at_ready")
        turns = sem("turns")

        x_t = x.rearrange("(n p) h -> p n h", p=P)
        x0_t = x0_rows[0:TOKENS, :].rearrange("(n p) h -> p n h", p=P)
        out_t = out[0:TOKENS, :].rearrange("(n p) h -> p n h", p=P)
        N_ROWS = NX + 1
        N_INIT = 2

        block = ctx.enter_context(nc.Block())

        def cond_weights(eng, half):
            eng.wait_ge(s_cond, 16)
            eng.wait_ge(s_wz, 1)
            with eng.Fori(0, NT) as i:
                c = eng.value_load(cond_sb[0:1, bass.ds(i * 2 + half, 1)], min_val=0, max_val=cond_w.shape[0] - 1)
                eng.dma_start(w_diag[half * C:(half + 1) * C, bass.ds(i, 1), half * C:(half + 1) * C],
                              cond_w[bass.ds(c, 1), :, :].rearrange("a c d -> c a d")).then_inc(s_wd, 16)

        @block.sync
        def _(sp):
            sp.dma_start(cond_sb[:], cond).then_inc(s_cond, 16)
            for n in range(NX):
                sp.dma_start(x_sb[:, n * TX:(n + 1) * TX, :], x_t[:, n * TX:(n + 1) * TX, :]).then_inc(s_x[n], 16)
            cond_weights(sp, 0)
            sp.dma_start(W[:, 0:WLEN], ffn_w[0]).then_inc(s_first, 16)
            for r in range(RING):
                sp.dma_start(BI[:, r * BLEN:(r + 1) * BLEN], ffn_b[r].partition_broadcast(P)).then_inc(s_first, 16)
            for n in range(NX):
                sp.wait_ge(s_x0c, (n + 1) * TX)
                sp.dma_start(x0_t[:, n * TX:(n + 1) * TX, :], x0_sb[:, n * TX:(n + 1) * TX, :]).then_inc(s_rows, 16)
            for r in range(1, RING):
                sp.dma_start(W[:, r * WLEN:(r + 1) * WLEN], ffn_w[r]).then_inc(s_first, 16)
            sp.wait_ge(s_meta, 1)
            sp.wait_ge(s_first, 16 * 2 * RING)

            def expert_for(s):
                buf = sp.value_load(meta[0:1, bass.ds(s, 1), 0], min_val=0, max_val=RING - 1)
                ex = sp.value_load(meta[0:1, bass.ds(s, 1), 2], min_val=0, max_val=E - 1)
                new = sp.value_load(meta[0:1, bass.ds(s, 1), 3], min_val=0, max_val=1)
                return buf, ex, new

            def load_w(buf, ex, new):
                sp.dma_start(W[:, bass.ds(buf * WLEN, WLEN)], ffn_w[bass.ds(ex, 1), :, :].rearrange("a p w -> p (a w)"),
                             cond=new).then_inc(loaded, 16)

            def load_b(buf, ex, new):
                sp.dma_start(BI[:, bass.ds(buf * BLEN, BLEN)],
                             ffn_b[bass.ds(ex, 1), :].to_broadcast([P, BLEN]), cond=new).then_inc(loaded, 16)

            for s in range(RING):
                which = expert_for(s)
                if s > 0:
                    sp.wait_ge(loaded, 32 * s)
                load_b(*which)
                load_w(*which)
            with sp.Fori(RING, SLOTS) as s:
                sp.wait_ge(zb_ready, s + (1 - RING))
                which = expert_for(s)
                sp.wait_ge(loaded, s * 32)
                load_b(*which)
                load_w(*which)
            sp.wait_ge(loaded, 32 * SLOTS)

        @block.gpsimd
        def _(pool):
            nc.gpsimd.memset(w_diag[:], 0.0).then_inc(s_wz, 1)
            nc.gpsimd.memset(ident[:], 0.0).then_inc(s_pool, 1)
            nc.gpsimd.memset(ones[:], 1.0).then_inc(s_pool, 1)
            nc.gpsimd.memset(earlier[:], 1.0).then_inc(s_pool, 1)
            pool.wait_ge(s_pool, 3)
            nc.gpsimd.affine_select(out=ident[:], in_=ident[:], compare_op=ALU.not_equal, fill=1.0, base=0,
                                    pattern=[[-1, P]], channel_multiplier=1).then_inc(s_const, 1)
            nc.gpsimd.affine_select(out=before[:], in_=ones[:], compare_op=ALU.is_gt, fill=0.0, base=0,
                                    pattern=[[1, P]], channel_multiplier=-1).then_inc(s_const, 1)
            nc.gpsimd.affine_select(out=earlier[:], in_=earlier[:], compare_op=ALU.is_gt, fill=0.0, base=0,
                                    pattern=[[1, E], [-1, E]], channel_multiplier=0).then_inc(s_const, 1)

            def iota(t, pattern, base=0, mult=0):
                nc.gpsimd.iota(t, pattern=pattern, base=base, channel_multiplier=mult,
                               allow_small_or_imprecise_dtypes=True).then_inc(s_const, 1)

            iota(row_id[:], [[1, P]], base=-P)
            iota(token_id[:], [[0, 2], [P, NT]], mult=1)
            iota(bounds[:], [[P, NB]])
            iota(slot_id[:], [[1, SLOTS]])
            iota(expert_id[:], [[1, E]])
            iota(rev_id[:], [[-1, E]], base=E)
            iota(fill_id[:], [[P, NT]])
            iota(pad_id[:], [[0, 1]], base=TOKENS, mult=1)
            iota(neg_pad[:], [[0, 1]], base=-TOKENS, mult=-1)

            pool.wait_ge(s_route, 1)
            pool.wait_ge(s_rows, 16 * N_ROWS)

            def gather(s):
                nc.gpsimd.tensor_copy(gather_at[:], tokens[:, bass.ds(s, 1)]).then_inc(at_ready, 1)

            def scatter(s):
                nc.gpsimd.tensor_copy(scatter_at[:], tokens[:, bass.ds(s, 1)]).then_inc(at_ready, 1)

            def start_gather():
                nc.gpsimd.indirect_dma_start(
                    out=xg[:], out_offset=None, in_=x0_rows[:, :],
                    in_offset=bass.IndirectOffsetOnAxis(ap=gather_at[:, 0:1], axis=0)).then_inc(gathered, 16)

            def start_scatter():
                nc.gpsimd.indirect_dma_start(
                    out=out[:, :], out_offset=bass.IndirectOffsetOnAxis(ap=scatter_at[:, 0:1], axis=0),
                    in_=zw[:], in_offset=None, compute_op=ALU.add).then_inc(scattered, 16)

            gather(0)
            pool.wait_ge(at_ready, 1)
            start_gather()
            pool.wait_ge(xT_made, 1)
            gather(1)
            pool.wait_ge(at_ready, 2)
            start_gather()
            pool.wait_ge(xT_made, 2)
            gather(2)
            pool.wait_ge(at_ready, 3)
            start_gather()
            pool.wait_ge(s_init, 16 * N_INIT)
            with pool.Fori(3, SLOTS) as s:
                pool.wait_ge(xT_made, s)
                gather(s)
                pool.wait_ge(at_ready, s * 2 - 2)
                pool.sem_inc(turns, 1)
                start_gather()
                pool.wait_ge(zw_ready, s - 2)
                scatter(s - 3)
                pool.wait_ge(at_ready, s * 2 - 1)
                pool.sem_inc(turns, 1)
                start_scatter()
                pool.wait_ge(scattered, s * 16 - 32)
            for s in range(SLOTS - 3, SLOTS):
                pool.wait_ge(zw_ready, s + 1)
                scatter(s)
                pool.wait_ge(at_ready, SLOTS + s + 1)
                start_scatter()
                pool.wait_ge(scattered, 16 * (s + 1))

        @block.scalar
        def _(act):
            act.dma_start(gw[:], gate_w).then_inc(s_gate, 16)
            act.dma_start(gb[:], gate_b.partition_broadcast(P)).then_inc(s_gate, 16)
            cond_weights(act, 1)
            act.wait_ge(s_x[0], 16)
            act.dma_start(x0_rows[TOKENS:TOKENS + P, :], x_sb[:, 0, :]).then_inc(s_rows, 16)
            for i in range(NT):
                act.wait_ge(s_x0, i + 1)
                nc.scalar.copy(x0_sb[:, i, :], ps_x0[i % 2][:]).then_inc(s_x0c, 1)
            for n in range(1, NX):
                act.wait_ge(s_x[n], 16)
            act.dma_start(out_t, x_sb[:]).then_inc(s_init, 16)
            act.dma_start(out[TOKENS:TOKENS + P, :], x_sb[:, 0, :]).then_inc(s_init, 16)
            act.wait_ge(s_gap, 1)
            nc.scalar.activation(egap[:], gap[:], ACT.Exp).then_inc(s_egap, 1)

            def copy_xT(s_plus_1):
                act.wait_ge(xT_made, s_plus_1)
                nc.scalar.copy(xT[:].rearrange("p k t -> p (k t)"), ps_xT[:]).then_inc(xT_ready, 1)

            def sigmoid(s_plus_1):
                act.wait_ge(g_ready, s_plus_1)
                nc.scalar.activation(sig[:], g[:], ACT.Sigmoid, scale=1.702).then_inc(sig_ready, 1)

            def copy_yT(s_plus_1):
                act.wait_ge(yT_made, s_plus_1)
                nc.scalar.copy(yT[:].rearrange("p k t -> p (k t)"), ps_yT[:]).then_inc(yT_ready, 1)

            def weigh(s, s_plus_1):
                act.wait_ge(zb_ready, s_plus_1)
                nc.scalar.mul(zw[:], zb[:], table[:, 2, bass.ds(s, 1)]).then_inc(zw_ready, 1)

            act.wait_ge(s_route, 1)
            copy_xT(1)
            sigmoid(1)
            act.wait_ge(lin_made, 1)
            copy_xT(2)
            copy_yT(1)
            sigmoid(2)
            act.wait_ge(lin_made, 2)
            copy_xT(3)
            weigh(0, 1)
            with act.Fori(2, SLOTS - 1) as s:
                act.wait_ge(z_made, s - 1)
                copy_yT(s)
                sigmoid(s + 1)
                act.wait_ge(lin_made, s + 1)
                copy_xT(s + 2)
                act.wait_ge(scattered, s * 16 - 16)
                weigh(s - 1, s)
            for s in (SLOTS - 1, SLOTS):
                act.wait_ge(z_made, s - 1)
                copy_yT(s)
                if s < SLOTS:
                    sigmoid(s + 1)
                act.wait_ge(scattered, s * 16 - 16)
                weigh(s - 1, s)

        @block.tensor
        def _(pe):
            pe.wait_ge(s_const, 3)
            pe.wait_ge(s_gate, 32)
            pe.wait_ge(s_wd, 16 * B)

            def condition(i):
                pe.wait_ge(s_x[i // TX], 16)
                if i >= 2:
                    pe.wait_ge(s_x0c, i - 1)
                nc.tensor.matmul(ps_x0[i % 2][:], w_diag[:, i, :], x_sb[:, i, :], start=True, stop=True).then_inc(s_x0, 1)

            def turn(i):
                pe.wait_ge(s_x0c, i + 1)
                if i >= 2:
                    pe.wait_ge(s_x0Tc, i - 1)
                for k in range(K):
                    last = nc.tensor.transpose(ps_x0T[i % 2][:, k * P:(k + 1) * P], x0_sb[:, i, k * P:(k + 1) * P], ident[:])
                last.then_inc(s_x0T, 1)

            def gate(i):
                pe.wait_ge(s_x0Tc, i + 1)
                for k in range(K):
                    last = nc.tensor.matmul(ps_log[:, i * E:(i + 1) * E], x0T[:, i % 2, k * P:(k + 1) * P], gw[:, k, :],
                                            start=(k == 0), stop=(k == K - 1))
                last.then_inc(s_log, 1)

            for i in range(NT + 2):
                if i < NT:
                    condition(i)
                if 1 <= i <= NT:
                    turn(i - 1)
                if i >= 2:
                    gate(i - 2)
            pe.wait_ge(s_mask, 1)
            nc.tensor.matmul(ps_rank[:], before[:], mask[:].rearrange("p n e -> p (n e)"), start=True, stop=False)
            for j in range(NT):
                last = nc.tensor.matmul(ps_rank[:, (j + 1) * E:].rearrange("p (n e) -> p n e", e=E), ones[:],
                                        mask[:, j:j + 1, :].to_broadcast([P, NT - j, E]), start=False, stop=(j == NT - 1))
            last.then_inc(s_rank, 1)
            for n in range(2):
                pe.wait_ge(s_hot, n + 1)
                for j in range(n * NT, (n + 1) * NT):
                    last = nc.tensor.matmul(ps_tab[:], row_hot[:, j, :], slot_hot[:, j, :, :].rearrange("p a s -> p (a s)"),
                                            start=(j == 0), stop=(j == NP - 1))
            last.then_inc(s_tab, 1)

            def turn_x(rows16):
                pe.wait_ge(gathered, rows16)
                for k in range(K):
                    last = nc.tensor.transpose(ps_xT[:, k * P:(k + 1) * P], xg[:, k * P:(k + 1) * P], ident[:])
                last.then_inc(xT_made, 1)

            def turn_y(s_plus_1):
                pe.wait_ge(y_ready, s_plus_1)
                for k in range(K):
                    last = nc.tensor.transpose(ps_yT[:, k * P:(k + 1) * P], y[:, k * P:(k + 1) * P], ident[:])
                last.then_inc(yT_made, 1)

            def product(dst, left, buf, at, done):
                for k in range(K):
                    last = nc.tensor.matmul(dst[:], left[:, k, :], W[:, bass.ds(buf * WLEN + (at + k * I), I)],
                                            start=(k == 0), stop=(k == K - 1))
                last.then_inc(done, 1)

            def expert_buffer(s, field):
                return pe.value_load(meta[0:1, bass.ds(s, 1), field], min_val=0, max_val=RING - 1)

            pe.wait_ge(s_route, 1)
            pe.wait_ge(s_meta, 1)
            pe.wait_ge(s_first, 16 * 2 * RING)
            turn_x(16)
            buf = expert_buffer(0, 0)
            pe.wait_ge(xT_ready, 1)
            pe.wait_ge(loaded, 32)
            product(ps_glu, xT, buf, GLU, glu_made)
            product(ps_lin, xT, buf, LIN, lin_made)
            turn_x(32)
            buf, last_buf = expert_buffer(1, 0), expert_buffer(1, 1)
            pe.wait_ge(xT_ready, 2)
            pe.wait_ge(loaded, 64)
            pe.wait_ge(g_ready, 1)
            product(ps_glu, xT, buf, GLU, glu_made)
            turn_y(1)
            product(ps_lin, xT, buf, LIN, lin_made)
            turn_x(48)
            pe.wait_ge(yT_ready, 1)
            product(ps_z, yT, last_buf, DOWN, z_made)
            with pe.Fori(2, SLOTS - 1) as s:
                buf = expert_buffer(s, 0)
                pe.wait_ge(xT_ready, s + 1)
                pe.wait_ge(loaded, s * 32 + 32)
                pe.wait_ge(g_ready, s)
                product(ps_glu, xT, buf, GLU, glu_made)
                turn_y(s)
                product(ps_lin, xT, buf, LIN, lin_made)
                turn_x(s * 16 + 32)
                last_buf = expert_buffer(s, 1)
                pe.wait_ge(yT_ready, s)
                pe.wait_ge(zb_ready, s - 1)
                product(ps_z, yT, last_buf, DOWN, z_made)
            s = SLOTS - 1
            buf = expert_buffer(s, 0)
            last_buf = expert_buffer(s, 1)
            pe.wait_ge(xT_ready, s + 1)
            pe.wait_ge(loaded, s * 32 + 32)
            pe.wait_ge(g_ready, s)
            product(ps_glu, xT, buf, GLU, glu_made)
            turn_y(s)
            product(ps_lin, xT, buf, LIN, lin_made)
            pe.wait_ge(yT_ready, s)
            pe.wait_ge(zb_ready, s - 1)
            product(ps_z, yT, last_buf, DOWN, z_made)
            turn_y(s + 1)
            pe.wait_ge(yT_ready, s + 1)
            pe.wait_ge(zb_ready, s)
            product(ps_z, yT, buf, DOWN, z_made)

        @block.vector
        def _(dve):
            v = nc.vector
            chain = [0]

            def link(ins):
                chain[0] += 1
                ins.then_inc(s_dve, 1)
                dve.wait_ge(s_dve, chain[0])

            for i in range(NT):
                dve.wait_ge(s_x0T, i + 1)
                if i >= 2:
                    dve.wait_ge(s_log, i - 1)
                v.tensor_copy(x0T[:, i % 2, :], ps_x0T[i % 2][:]).then_inc(s_x0Tc, 1)

            dve.wait_ge(s_log, NT)
            dve.wait_ge(s_const, 12)
            dve.wait_ge(s_gate, 32)
            te = [P, NT, E]
            link(v.tensor_tensor(logits[:], ps_log[:].rearrange("p (n e) -> p n e", e=E),
                                 gb[:].unsqueeze(1).to_broadcast(te), ALU.add))
            rev = rev_id[:].unsqueeze(1).to_broadcast(te)
            src = logits
            for c in range(2):
                link(v.tensor_reduce(best[:, c, :], src[:], AX_X, ALU.max))
                link(v.tensor_tensor(hit[:], src[:], best[:, c, :].unsqueeze(2).to_broadcast(te), ALU.is_equal))
                link(v.tensor_tensor(key[:], hit[:], rev, ALU.mult))
                link(v.tensor_reduce(pick[:, c, :], key[:], AX_X, ALU.max))
                link(v.tensor_tensor(chosen[:, c, :, :], rev, pick[:, c, :].unsqueeze(2).to_broadcast(te), ALU.is_equal))
                if c == 0:
                    link(v.scalar_tensor_tensor(out=rest[:], in0=chosen[:, 0, :, :], scalar=FLOOR, in1=logits[:],
                                                op0=ALU.mult, op1=ALU.add))
                    src = rest
            v.tensor_tensor(gap[:], best[:, 1, :], best[:, 0, :], ALU.subtract).then_inc(s_gap, 1)
            link(v.memset(mask[:, NT, :], 0.0))
            v.tensor_tensor(mask[:, 0:NT, :], chosen[:, 0, :, :], chosen[:, 1, :, :], ALU.add).then_inc(s_mask, 1)
            dve.wait_ge(s_egap, 1)
            link(v.tensor_scalar(den[:], egap[:], 1.0, None, ALU.add))
            link(v.reciprocal(share[:, 0, :], den[:]))
            link(v.tensor_tensor(share[:, 1, :], share[:, 0, :], egap[:], ALU.mult))
            dve.wait_ge(s_rank, 1)
            een = [P, E, NT]
            link(v.tensor_tensor(full[:], ps_rank[:, NT * E:].unsqueeze(2).to_broadcast(een),
                                 fill_id[:].unsqueeze(1).to_broadcast(een), ALU.is_gt))
            link(v.tensor_reduce(tiles_of[:], full[:], AX_X, ALU.add))
            link(v.tensor_tensor(bef[:], earlier[:], tiles_of[:].unsqueeze(1).to_broadcast([P, E, E]), ALU.mult))
            link(v.tensor_reduce(base[:], bef[:], AX_X, ALU.add))
            link(v.tensor_scalar(base_rows[:], base[:], float(P), None, ALU.mult))
            link(v.tensor_tensor(place_e[:], ps_rank[:, 0:NT * E].rearrange("p (n e) -> p n e", e=E),
                                 base_rows[:].unsqueeze(1).to_broadcast(te), ALU.add))
            link(v.tensor_tensor(place_k[:], chosen[:], place_e[:].unsqueeze(1).to_broadcast([P, 2, NT, E]), ALU.mult))
            link(v.tensor_reduce(place[:], place_k[:].rearrange("p c n e -> p (c n) e"), AX_X, ALU.add))
            link(v.tensor_tensor(past[:], place[:].unsqueeze(2).to_broadcast([P, NP, NB]),
                                 bounds[:].unsqueeze(1).to_broadcast([P, NP, NB]), ALU.is_ge))
            link(v.tensor_reduce(count[:], past[:], AX_X, ALU.add))
            link(v.scalar_tensor_tensor(out=row_of[:], in0=count[:], scalar=float(-P), in1=place[:],
                                        op0=ALU.mult, op1=ALU.add))
            dve.wait_ge(s_rows, 16 * N_ROWS)
            share_f = share[:].rearrange("p c n -> p (c n)")
            for c in range(2):
                h = slice(c * NT, (c + 1) * NT)
                ns = [P, NT, SLOTS]
                v.tensor_tensor(row_hot[:, h, :], row_of[:, h].unsqueeze(2).to_broadcast([P, NT, P]),
                                row_id[:].unsqueeze(1).to_broadcast([P, NT, P]), ALU.is_equal)
                link(v.tensor_tensor(slot_hot[:, h, 0, :], past[:, h, 0:SLOTS], past[:, h, 1:NB], ALU.subtract))
                link(v.tensor_tensor(slot_hot[:, h, 1, :], slot_hot[:, h, 0, :],
                                     token_id[:, h].unsqueeze(2).to_broadcast(ns), ALU.mult))
                v.tensor_tensor(slot_hot[:, h, 2, :], slot_hot[:, h, 0, :],
                                share_f[:, h].unsqueeze(2).to_broadcast(ns), ALU.mult).then_inc(s_hot, 1)
            es = [1, SLOTS, E]
            link(v.tensor_scalar(used[:], tiles_of[0:1, :], 0.0, None, ALU.is_gt))
            link(v.tensor_tensor(begun[:], slot_id[0:1, :].unsqueeze(2).to_broadcast(es),
                                 base[0:1, :].unsqueeze(1).to_broadcast(es), ALU.is_ge))
            link(v.tensor_tensor(begun[:], begun[:], used[:].unsqueeze(1).to_broadcast(es), ALU.mult))
            link(v.memset(order[:, 0:1], 0.0))
            link(v.tensor_reduce(order[:, 1:], begun[:], AX_X, ALU.add))
            link(v.tensor_tensor(begun_id[:], begun[:], expert_id[0:1, :].unsqueeze(1).to_broadcast(es), ALU.mult))
            link(v.tensor_reduce(expert_of[:], begun_id[:], AX_X, ALU.max))
            starts, guessed, low, third, sixth, ring, a, b = (m[:, n, :] for n in range(8))
            link(v.tensor_tensor(starts, order[:, 1:], order[:, 0:SLOTS], ALU.subtract))
            link(v.scalar_tensor_tensor(out=guessed, in0=expert_of[:], scalar=1.0, in1=order[:, 1:],
                                        op0=ALU.add, op1=ALU.is_equal))
            link(v.tensor_scalar(low, expert_of[:], float(RING), None, ALU.is_lt))
            link(v.tensor_tensor(a, guessed, low, ALU.mult))
            link(v.tensor_tensor(b, a, starts, ALU.mult))
            link(v.tensor_scalar(third, order[:, 1:], float(RING), float(-RING), ALU.is_gt, ALU.mult))
            link(v.tensor_scalar(sixth, order[:, 1:], float(2 * RING), float(-RING), ALU.is_gt, ALU.mult))
            link(v.tensor_tensor(ring, third, sixth, ALU.add))
            link(v.scalar_tensor_tensor(out=meta[:, 0:SLOTS, 0], in0=order[:, 1:], scalar=-1.0, in1=ring,
                                        op0=ALU.add, op1=ALU.add))
            v.tensor_copy(meta[:, 0:1, 1], order[:, 0:1])
            v.scalar_tensor_tensor(out=meta[:, 1:SLOTS + 1, 1], in0=order[:, 1:], scalar=-1.0, in1=ring,
                                   op0=ALU.add, op1=ALU.add)
            v.tensor_copy(meta[:, 0:SLOTS, 2], expert_of[:])
            v.tensor_tensor(meta[:, 0:SLOTS, 3], starts, b, ALU.subtract).then_inc(s_meta, 1)
            dve.wait_ge(s_tab, 1)
            link(v.tensor_copy(table[:].rearrange("p a s -> p (a s)"), ps_tab[:]))
            link(v.scalar_tensor_tensor(out=fill[:], in0=table[:, 0, :], scalar=neg_pad[:, 0:1], in1=table[:, 1, :],
                                        op0=ALU.mult, op1=ALU.add))
            v.tensor_scalar(tokens[:], fill[:], pad_id[:, 0:1], None, ALU.add).then_inc(s_route, 1)

            def bias(buf, at, n):
                return BI[:, bass.ds(buf * BLEN + at, n)]

            def gated(buf, s_plus_1, parts):
                dve.wait_ge(glu_made, s_plus_1)
                dve.wait_ge(loaded, s_plus_1 * 32)
                v.tensor_tensor(g[:], ps_glu[:], bias(buf, BG, I), ALU.add).then_inc(g_ready, 1)
                dve.wait_ge(lin_made, s_plus_1)
                v.tensor_tensor(lin[:], ps_lin[:], bias(buf, BL, I), ALU.add).then_inc(part_ready, 1)
                dve.wait_ge(sig_ready, s_plus_1)
                v.tensor_tensor(gs[:], g[:], sig[:], ALU.mult).then_inc(part_ready, 1)
                dve.wait_ge(part_ready, parts)
                v.scalar_tensor_tensor(out=y[:], in0=lin[:], scalar=1.0, in1=gs[:],
                                       op0=ALU.add, op1=ALU.mult).then_inc(y_ready, 1)

            def down(buf, s_plus_1):
                dve.wait_ge(z_made, s_plus_1)
                v.tensor_tensor(zb[:], ps_z[:], bias(buf, BD, H), ALU.add).then_inc(zb_ready, 1)

            def expert_buffer(s, field):
                return dve.value_load(meta[0:1, bass.ds(s, 1), field], min_val=0, max_val=RING - 1)

            dve.wait_ge(s_meta, 1)
            dve.wait_ge(s_first, 16 * 2 * RING)
            gated(expert_buffer(0, 0), 1, 2)
            dve.wait_ge(yT_made, 1)
            gated(expert_buffer(1, 0), 2, 4)
            down(expert_buffer(1, 1), 1)
            with dve.Fori(2, SLOTS) as s:
                buf = expert_buffer(s, 0)
                last_buf = expert_buffer(s, 1)
                dve.wait_ge(yT_made, s)
                gated(buf, s + 1, s * 2 + 2)
                dve.wait_ge(zw_ready, s - 1)
                down(last_buf, s)
            dve.wait_ge(zw_ready, SLOTS - 1)
            down(expert_buffer(SLOTS, 1), SLOTS)


def kernel(x, itok_B_1_198, L0_cond_weights, L0_ffn_gate_w, L0_ffn_gate_b, L0_ffn_w1, L0_ffn_b1, L0_ffn_w2, L0_ffn_b2):
    import numpy as np
    import concourse.bacc as bacc
    from concourse.bass_utils import run_bass_kernel_spmd

    B, C, H = x.shape
    E = L0_ffn_w1.shape[0]
    K = H // P

    def by_rows(w):
        w = np.asarray(w)
        return w.transpose(0, 2, 1).reshape(E, K, P, w.shape[1]).transpose(0, 2, 1, 3).reshape(E, P, K * w.shape[1])

    w1, b1 = np.asarray(L0_ffn_w1), np.asarray(L0_ffn_b1)
    arrays = {
        "x": np.asarray(x).reshape(B * C, H),
        "cond": np.asarray(itok_B_1_198).reshape(1, B),
        "cond_w": np.asarray(L0_cond_weights),
        "gate_w": np.asarray(L0_ffn_gate_w).T.reshape(K, P, E).transpose(1, 0, 2),
        "gate_b": np.asarray(L0_ffn_gate_b),
        "ffn_w": np.concatenate([by_rows(w1[:, 0::2]), by_rows(w1[:, 1::2]), by_rows(L0_ffn_w2)], axis=2),
        "ffn_b": np.concatenate([b1[:, 0::2], b1[:, 1::2], np.asarray(L0_ffn_b2)], axis=1),
    }
    arrays = {k: np.ascontiguousarray(a) for k, a in arrays.items()}
    nc = bacc.Bacc("TRN2", target_bir_lowering=False, num_devices=1)
    ins = [nc.dram_tensor(n, a.shape, mybir.dt.from_np(a.dtype), kind="ExternalInput").ap() for n, a in arrays.items()]
    x0_rows = nc.dram_tensor("x0_rows", (B * C + P, H), F32, kind="Internal").ap()
    out = nc.dram_tensor("out", (B * C + P, H), F32, kind="ExternalOutput").ap()
    adaln_moe_kernel(nc, *ins, x0_rows, out)
    r = run_bass_kernel_spmd(nc, [arrays], core_ids=[0])
    return r.results[0]["out"][:B * C].reshape(B, C, H)
```

```python
from contextlib import ExitStack

import concourse.bass as bass
from concourse import mybir

P = 128
ALU = mybir.AluOpType
ACT = mybir.ActivationFunctionType
F32 = mybir.dt.float32
F32R = mybir.dt.float32r
BF16 = mybir.dt.bfloat16
I32 = mybir.dt.int32
AX_X = mybir.AxisListType.X

RING = 2
B_RING = 3
CHUNKS = 6
FLOOR = -3.0e38


def adaln_moe_kernel(nc, x, cond, cond_w, gate_w, gate_b, ffn_w, ffn_b, cond_rows, x0_rows, out):
    TOKENS, H = x.shape
    B = cond.shape[0]
    C = TOKENS // B
    E = ffn_w.shape[0]
    K = H // P
    I = H
    NT = TOKENS // P
    SLOTS = (2 * TOKENS + E * (P - 1)) // P
    NS = SLOTS + 1
    NP = 2 * NT
    GLU, LIN, DOWN = 0, K * I, 2 * K * I
    WLEN = 2 * K * I + K * H
    BG, BL, BD = 0, I, 2 * I
    BLEN = 2 * I + H
    NX = 8
    TX = NT // NX
    NG = 4
    TG = NT // NG
    RANK_AT = 4
    NPT = 3
    PIECE = WLEN // CHUNKS
    A_LOADS = 16 * CHUNKS // 2
    B_LOADS = 16 * CHUNKS // 2 + 16
    E_BITS, S_BITS = (E - 1).bit_length(), SLOTS.bit_length()
    AT_A = E_BITS
    AT_B = AT_A + 1
    AT_LIVE = AT_B + 1
    AT_FIRST = AT_LIVE + 1
    AT_BEFORE = AT_FIRST + S_BITS
    DVE_START = 3
    assert B == 2 * NT and C == 64 and ffn_w.shape[2] == WLEN and ffn_b.shape[1] == BLEN

    with ExitStack() as ctx:
        def sb(name, shape, dt=F32):
            return ctx.enter_context(nc.sbuf_tensor(name, shape, dt))

        def psum(name, shape):
            return ctx.enter_context(nc.psum_tensor(name, shape, F32))

        def sem(name):
            return ctx.enter_context(nc.semaphore(name))

        ident = sb("ident", [P, P])
        before = sb("before", [P, P], BF16)
        ones = sb("ones", [P, P], BF16)
        row_id = sb("row_id", [P, P])
        slot_id = sb("slot_id", [P, NS])
        rev_id = sb("rev_id", [P, E])
        fill_id = sb("fill_id", [P, NT])
        earlier = sb("earlier", [P, E, E])
        pad_id = sb("pad_id", [P, 1])
        cond_sb = sb("cond_sb", [B, 1], I32)
        w_diag = sb("w_diag", [P, NT, P])
        gw = sb("gw", [P, K, E])
        gw_split = sb("gw_split", [P, K, 2, E], F32R)
        gb = sb("gb", [P, E])
        gated_x = sb("gated_x", [P, NT, 2, E])
        xg8 = sb("xg8", [P, NT, E])
        logits = sb("logits", [P, NT, E])
        rest = sb("rest", [P, NT, E])
        hit = sb("hit", [P, NT, E])
        key = sb("key", [P, NT, E])
        best = sb("best", [P, 2, NT])
        pick = sb("pick", [P, 2, NT])
        chosen = sb("chosen", [P, 2, NT, E])
        gap = sb("gap", [P, NT])
        egap = sb("egap", [P, NT])
        den = sb("den", [P, NT])
        den_a = sb("den_a", [P, NT])
        share = sb("share", [P, NP])
        share_hi = sb("share_hi", [P, NP], F32R)
        mask = sb("mask", [P, NT + 1, E], BF16)
        full = sb("full", [P, E, NT])
        tiles_of = sb("tiles_of", [P, E])
        bef = sb("bef", [P, E, E])
        base = sb("base", [P, E])
        base_rows = sb("base_rows", [P, E])
        place_e = sb("place_e", [P, NT, E])
        place_k = sb("place_k", [P, 2, NT, E])
        place = sb("place", [P, NP])
        place_i = sb("place_i", [P, NP], I32)
        slot_of = sb("slot_of", [P, NP], I32)
        row_of = sb("row_of", [P, NP], I32)
        values = sb("values", [P, NP, 3])
        slot_hot = sb("slot_hot", [P, NP, NS])
        with ExitStack() as early:
            cond_mats = early.enter_context(nc.sbuf_tensor("cond_mats", [B, C * C], F32))
        row_hot = sb("row_hot", [P, NP, P], F32R)
        table = sb("table", [P, 3, NS])
        fill = sb("fill", [P, NS])
        tokens = sb("tokens", [P, NS], I32)
        share_of = sb("share_of", [P, NS])
        ends = sb("ends", [1, E])
        over = sb("over", [1, NS, E])
        ended = sb("ended", [1, NS])
        expert_of = sb("expert_of", [1, NS])
        splits = sb("splits", [1, 2, NS])
        lasts = sb("lasts", [1, E])
        turn_a = sb("turn_a", [1, E])
        turn_b = sb("turn_b", [1, E])
        at_turn = sb("at_turn", [1, NS, E - 1])
        meta = sb("meta", [1, NS], I32)
        packed = sb("packed", [1, NS])
        live = sb("live", [1, NS])
        first_of = sb("first_of", [1, NS])
        extra_i = sb("extra_i", [1, 1], I32)
        BI = sb("BI", [P, B_RING * BLEN])
        raw = sb("raw", [P, WLEN])
        with ExitStack() as early:
            early.enter_context(nc.sbuf_tensor("first_half", [P, 2 * WLEN], F32))
            x_sb = early.enter_context(nc.sbuf_tensor("x_sb", [P, NT, H], F32))
            with ExitStack() as first:
                x_hi = first.enter_context(nc.sbuf_tensor("x_hi", [P, NPT, K * P], F32R))
                x_lo = first.enter_context(nc.sbuf_tensor("x_lo", [P, NPT, K * P], F32R))
            slot_values = early.enter_context(nc.sbuf_tensor("slot_values", [P, NP, 3, NS], F32R))
        W = sb("W", [P, RING * 2 * WLEN], F32R)
        with ExitStack() as early:
            x0_sb = early.enter_context(nc.sbuf_tensor("x0_sb", [P, 2 * TG, H], F32))
        xg = sb("xg", [P, H])
        xT_hi = sb("xT_hi", [P, K * P], F32R)
        xT_lo = sb("xT_lo", [P, K * P], F32R)
        g = sb("g", [P, I])
        lin = sb("lin", [P, I])
        sig = sb("sig", [P, I])
        gs = sb("gs", [P, I])
        y = sb("y", [P, I])
        yT_hi = sb("yT_hi", [P, K * P], F32R)
        yT_lo = sb("yT_lo", [P, K * P], F32R)
        zb = sb("zb", [P, H])
        zw = sb("zw", [P, H])
        gather_at = sb("gather_at", [P, 1], I32)
        scatter_at = sb("scatter_at", [P, 1], I32)

        ps_glu = psum("ps_glu", [P, I])
        ps_lin = psum("ps_lin", [P, I])
        ps_z = psum("ps_z", [P, H])
        ps_xT = psum("ps_xT", [P, K * P])
        ps_yT = psum("ps_yT", [P, K * P])
        ps_gate = psum("ps_gate", [P, NT * 2 * E])
        ps_rank = psum("ps_rank", [P, (NT + 1) * E])
        ps_log = psum("ps_log", [P, NT * E])
        ps_x0 = [ps_glu, ps_lin]
        ps_turn = [ps_xT, ps_yT, ps_z]
        ps_tab = ps_gate

        s_cond = sem("s_cond")
        s_gate = sem("s_gate")
        s_x = [sem(f"s_x_part{n}") for n in range(NX)]
        s_wz = sem("s_wz")
        s_wg = sem("s_wg")
        s_wr = sem("s_wr")
        s_wd = sem("s_wd")
        s_const = sem("s_const")
        s_gws = sem("s_gws")
        s_turn = sem("s_turn")
        s_hi = sem("s_hi")
        s_lo = sem("s_lo")
        s_gx = sem("s_gx")
        s_xg8 = sem("s_xg8")
        s_x0 = sem("s_x0")
        s_x0c = sem("s_x0c")
        s_log = sem("s_log")
        s_rows = [sem(f"s_rows{n}") for n in range(NG)]
        s_pad = sem("s_pad")
        s_init = sem("s_init")
        s_gap = sem("s_gap")
        s_egap = sem("s_egap")
        s_mask = sem("s_mask")
        s_rank = sem("s_rank")
        s_slot_hot = sem("s_slot_hot")
        s_row_hot = sem("s_row_hot")
        s_hot = sem("s_hot")
        s_hot2 = sem("s_hot2")
        s_tab = sem("s_tab")
        s_route = sem("s_route")
        s_meta = sem("s_meta")
        s_dve = sem("s_dve")
        s_pool = sem("s_pool")
        loaded_a = sem("loaded_a")
        loaded_b = sem("loaded_b")
        gathered = sem("gathered")
        xT_made = sem("xT_made")
        xT_rounded = sem("xT_rounded")
        xT_ready = sem("xT_ready")
        split_hi = sem("split_hi")
        split_dve = sem("split_dve")
        split_pool = sem("split_pool")
        glu_made = sem("glu_made")
        lin_made = sem("lin_made")
        g_ready = sem("g_ready")
        sig_ready = sem("sig_ready")
        part_ready = sem("part_ready")
        y_ready = sem("y_ready")
        yT_made = sem("yT_made")
        yT_rounded = sem("yT_rounded")
        yT_ready = sem("yT_ready")
        z_made = sem("z_made")
        zb_ready = sem("zb_ready")
        zw_ready = sem("zw_ready")
        scattered = sem("scattered")
        at_ready = sem("at_ready")
        turns = sem("turns")

        x_t = x.rearrange("(n p) h -> p n h", p=P)
        x0_t = x0_rows[0:TOKENS, :].rearrange("(n p) h -> p n h", p=P)
        out_t = out[0:TOKENS, :].rearrange("(n p) h -> p n h", p=P)
        w_parts = ffn_w.rearrange("e p (c n) -> e p c n", c=CHUNKS)
        raw_parts = raw[:].rearrange("p (c n) -> p c n", c=CHUNKS)
        pairs = cond_rows.rearrange("(n two) (c d) -> two c n d", two=2, d=C)
        N_CONST = 12

        def word_of(eng, s):
            return eng.value_load(meta[0:1, bass.ds(s, 1)], min_val=0, max_val=(E << AT_BEFORE) - 1)

        def bits(eng, word, at, n):
            return eng.snap((word >> at) & ((1 << n) - 1), min_val=0, max_val=(1 << n) - 1)

        def expert(eng, word):
            return bits(eng, word, 0, E_BITS)

        def expert_before(eng, word):
            return bits(eng, word, AT_BEFORE, E_BITS)

        def place_of_w(eng, e):
            return eng.snap((e & (RING - 1)) * (2 * WLEN), min_val=0, max_val=(RING - 1) * 2 * WLEN)

        def next_place_of_w(eng, e):
            return eng.snap(((e + 1) & (RING - 1)) * (2 * WLEN), min_val=0, max_val=(RING - 1) * 2 * WLEN)

        def place_of_b(eng, e):
            return eng.snap((e % B_RING) * BLEN, min_val=0, max_val=(B_RING - 1) * BLEN)

        def slots_in_use(eng):
            return eng.value_load(extra_i[0:1, 0:1], min_val=0, max_val=SLOTS - NT) + NT

        def spread_values(eng, c):
            h = slice(c * NT, (c + 1) * NT)
            nas = [P, NT, 3, NS]
            return eng.tensor_tensor(slot_values[:, h, :, :], slot_hot[:, h, :].unsqueeze(2).to_broadcast(nas),
                                     values[:, h, :].unsqueeze(3).to_broadcast(nas), ALU.mult)

        block = ctx.enter_context(nc.Block())

        @block.sync
        def _(sp):
            sp.dma_start(cond_sb[:], cond).then_inc(s_cond, 16)
            for n in range(NX):
                sp.dma_start(x_sb[:, n * TX:(n + 1) * TX, :], x_t[:, n * TX:(n + 1) * TX, :]).then_inc(s_x[n], 16)
            sp.wait_ge(s_wg, 16)
            sp.dma_start(cond_rows, cond_mats[:]).then_inc(s_wr, 16)
            sp.wait_ge(s_wr, 16)
            sp.wait_ge(s_wz, 1)
            for half in range(2):
                rows = slice(half * C, (half + 1) * C)
                sp.dma_start(w_diag[rows, :, rows], pairs[half]).then_inc(s_wd, 16)

            def load(e, c):
                half, n, of = [(loaded_a, c, A_LOADS), (loaded_b, c - CHUNKS // 2, B_LOADS)][c >= CHUNKS // 2]
                if e * of + n > 0:
                    sp.wait_ge(half, e * of + n * 16)
                sp.dma_start(raw_parts[:, c, :], w_parts[e, :, c, :]).then_inc(half, 16)

            def load_biases(e):
                at = (e % B_RING) * BLEN
                sp.wait_ge(loaded_b, e * B_LOADS + B_LOADS - 16)
                sp.dma_start(BI[:, at:at + BLEN], ffn_b[e].partition_broadcast(P)).then_inc(loaded_b, 16)

            for c in range(CHUNKS):
                load(0, c)
            load_biases(0)
            for n in range(NX):
                sp.wait_ge(s_x[n], 16)
            sp.dma_start(out_t, x_sb[:]).then_inc(s_init, 16)
            sp.dma_start(out[TOKENS:TOKENS + P, :], x_sb[:, 0, :]).then_inc(s_init, 16)
            for e in range(1, E):
                for c in range(CHUNKS):
                    if e == 1:
                        sp.wait_ge(split_pool, 2)
                    elif c < 4:
                        sp.wait_ge(split_dve, DVE_START + 4 * (e - 2) + c + 1)
                    else:
                        sp.wait_ge(split_pool, 2 * (e - 1) + c - 3)
                    load(e, c)
                load_biases(e)
            sp.wait_ge(loaded_a, A_LOADS * E)
            sp.wait_ge(loaded_b, B_LOADS * E)
            sp.wait_ge(s_init, 32)

        @block.gpsimd
        def _(pool):
            nc.gpsimd.memset(ident[:], 0.0).then_inc(s_pool, 1)
            nc.gpsimd.memset(ones[:], 1.0).then_inc(s_pool, 1)
            nc.gpsimd.memset(earlier[:], 1.0).then_inc(s_pool, 1)
            pool.wait_ge(s_pool, 3)
            nc.gpsimd.affine_select(out=ident[:], in_=ident[:], compare_op=ALU.not_equal, fill=1.0, base=0,
                                    pattern=[[-1, P]], channel_multiplier=1).then_inc(s_const, 1)
            pool.wait_ge(s_cond, 16)
            nc.gpsimd.indirect_dma_start(
                out=cond_mats[:], out_offset=None, in_=cond_w.rearrange("s c d -> s (c d)"),
                in_offset=bass.IndirectOffsetOnAxis(ap=cond_sb[:, 0:1], axis=0)).then_inc(s_wg, 16)
            nc.gpsimd.memset(w_diag[:], 0.0).then_inc(s_wz, 1)
            nc.gpsimd.affine_select(out=before[:], in_=ones[:], compare_op=ALU.is_gt, fill=0.0, base=0,
                                    pattern=[[1, P]], channel_multiplier=-1).then_inc(s_const, 1)
            nc.gpsimd.affine_select(out=earlier[:], in_=earlier[:], compare_op=ALU.is_gt, fill=0.0, base=0,
                                    pattern=[[1, E], [-1, E]], channel_multiplier=0).then_inc(s_const, 1)

            def iota(t, pattern, base=0, mult=0):
                nc.gpsimd.iota(t, pattern=pattern, base=base, channel_multiplier=mult,
                               allow_small_or_imprecise_dtypes=True).then_inc(s_const, 1)

            iota(row_id[:], [[1, P]])
            iota(values[:, :, 0], [[0, 2], [P, NT]], base=1, mult=1)
            iota(slot_id[:], [[1, NS]])
            iota(rev_id[:], [[-1, E]], base=E)
            iota(fill_id[:], [[P, NT]])
            iota(pad_id[:], [[0, 1]], base=TOKENS + 1, mult=1)

            for c in range(CHUNKS):
                at = c * PIECE
                pool.wait_ge(split_hi, c + 1)
                last = nc.gpsimd.tensor_tensor(W[:, WLEN + at:WLEN + at + PIECE], raw[:, at:at + PIECE],
                                               W[:, at:at + PIECE].bitcast(F32), ALU.subtract)
            last.then_inc(split_pool, 2)
            pool.wait_ge(s_slot_hot, 1)
            spread_values(nc.gpsimd, 1).then_inc(s_hot2, 1)
            pool.wait_ge(s_route, 1)
            for n in range(NG):
                pool.wait_ge(s_rows[n], 16)
            pool.wait_ge(s_pad, 16)

            def gather(s):
                nc.gpsimd.tensor_copy(gather_at[:], tokens[:, bass.ds(s, 1)]).then_inc(at_ready, 1)

            def scatter(s):
                nc.gpsimd.tensor_copy(scatter_at[:], tokens[:, bass.ds(s, 1)]).then_inc(at_ready, 1)

            def start_gather():
                nc.gpsimd.indirect_dma_start(
                    out=xg[:], out_offset=None, in_=x0_rows[:, :],
                    in_offset=bass.IndirectOffsetOnAxis(ap=gather_at[:, 0:1], axis=0)).then_inc(gathered, 16)

            def start_scatter():
                nc.gpsimd.indirect_dma_start(
                    out=out[:, :], out_offset=bass.IndirectOffsetOnAxis(ap=scatter_at[:, 0:1], axis=0),
                    in_=zw[:], in_offset=None, compute_op=ALU.add).then_inc(scattered, 16)

            def split_down(s):
                word = word_of(pool, s)
                with pool.If(bits(pool, word, AT_B, 1)):
                    e = expert(pool, word)
                    to = next_place_of_w(pool, e)
                    for c in (4, 5):
                        pool.wait_ge(split_hi, e * CHUNKS + (CHUNKS + c + 1))
                        nc.gpsimd.tensor_tensor(W[:, bass.ds(to + (WLEN + c * PIECE), PIECE)], raw[:, c * PIECE:(c + 1) * PIECE],
                                                W[:, bass.ds(to + c * PIECE, PIECE)].bitcast(F32),
                                                ALU.subtract).then_inc(split_pool, 1)

            for s in range(3):
                if s > 0:
                    pool.wait_ge(xT_made, s)
                gather(s)
                pool.wait_ge(at_ready, s + 1)
                start_gather()
            pool.wait_ge(s_meta, 1)
            split_down(0)
            pool.wait_ge(s_init, 32)
            with pool.Fori(3, SLOTS) as s:
                word = word_of(pool, s)
                with pool.If(bits(pool, word, AT_LIVE, 1)):
                    pool.wait_ge(xT_made, s)
                    gather(s)
                    pool.wait_ge(at_ready, s * 2 - 2)
                    pool.sem_inc(turns, 1)
                    start_gather()
                    pool.wait_ge(zw_ready, s - 2)
                    scatter(s - 3)
                    pool.wait_ge(at_ready, s * 2 - 1)
                    pool.sem_inc(turns, 1)
                    start_scatter()
                    split_down(s - 2)
                    pool.wait_ge(scattered, s * 16 - 32)
            n_slots = slots_in_use(pool)
            pool.wait_ge(xT_made, n_slots)
            gather(n_slots)
            pool.wait_ge(at_ready, n_slots * 2 - 2)
            pool.sem_inc(turns, 1)
            start_gather()
            split_down(n_slots - 2)
            for back in (3, 2, 1):
                pool.wait_ge(zw_ready, n_slots + (1 - back))
                scatter(n_slots - back)
                pool.wait_ge(at_ready, n_slots * 2 + (2 - back))
                pool.sem_inc(turns, 1)
                start_scatter()
                pool.wait_ge(scattered, n_slots * 16 + 16 * (1 - back))

        @block.scalar
        def _(act):
            act.dma_start(gw[:], gate_w).then_inc(s_gate, 16)
            act.dma_start(gb[:], gate_b.partition_broadcast(P)).then_inc(s_gate, 16)
            for i in range(NT):
                act.wait_ge(s_turn, i + 1)
                if i >= NPT:
                    act.wait_ge(s_gx, i - NPT + 1)
                nc.scalar.copy(x_hi[:, i % NPT, :], ps_turn[i % NPT][:]).then_inc(s_hi, 1)
            act.wait_ge(loaded_a, A_LOADS)
            act.wait_ge(loaded_b, B_LOADS)
            for c in range(CHUNKS):
                nc.scalar.copy(W[:, c * PIECE:(c + 1) * PIECE], raw[:, c * PIECE:(c + 1) * PIECE]).then_inc(split_hi, 1)
            act.wait_ge(s_x[0], 16)
            act.dma_start(x0_rows[TOKENS:TOKENS + P, :], x_sb[:, 0, :]).then_inc(s_pad, 16)

            def exp_gap():
                act.wait_ge(s_gap, 1)
                nc.scalar.activation(egap[:], gap[:], ACT.Exp).then_inc(s_egap, 1)
                nc.scalar.activation(den_a[:], gap[:], ACT.Sigmoid)

            for i in range(NT):
                if i == RANK_AT + 1:
                    exp_gap()
                act.wait_ge(s_x0, i + 1)
                if i >= 2 * TG and i % TG == 0:
                    act.wait_ge(s_rows[i // TG - 2], 16)
                nc.scalar.copy(x0_sb[:, i % (2 * TG), :], ps_x0[i % 2][:]).then_inc(s_x0c, 1)
                if i % TG == TG - 1:
                    n, at = i // TG, (i // TG) % 2 * TG
                    act.wait_ge(s_x0c, i + 1)
                    act.dma_start(x0_t[:, n * TG:(n + 1) * TG, :], x0_sb[:, at:at + TG, :]).then_inc(s_rows[n], 16)

            def copy_xT(s_plus_1):
                act.wait_ge(xT_made, s_plus_1)
                nc.scalar.copy(xT_hi[:], ps_xT[:]).then_inc(xT_rounded, 1)

            def sigmoid(s_plus_1):
                act.wait_ge(g_ready, s_plus_1)
                nc.scalar.activation(sig[:], g[:], ACT.Sigmoid, scale=1.702).then_inc(sig_ready, 1)

            def copy_yT(s_plus_1):
                act.wait_ge(yT_made, s_plus_1)
                nc.scalar.copy(yT_hi[:], ps_yT[:]).then_inc(yT_rounded, 1)

            def round_chunks(s, word, flag, chunks):
                with act.If(bits(act, word, flag, 1)):
                    e = expert(act, word)
                    to = next_place_of_w(act, e)
                    if 0 in chunks:
                        act.wait_ge(loaded_a, e * A_LOADS + 2 * A_LOADS)
                        if s is not zero:
                            act.wait_ge(lin_made, s)
                    if 3 in chunks:
                        act.wait_ge(loaded_b, e * B_LOADS + 2 * B_LOADS)
                    act.wait_ge(s_init, 32)
                    for c in chunks:
                        if c == 4 and s is not zero:
                            act.wait_ge(z_made, bits(act, word, AT_FIRST, S_BITS))
                        nc.scalar.copy(W[:, bass.ds(to + c * PIECE, PIECE)], raw[:, c * PIECE:(c + 1) * PIECE]).then_inc(split_hi, 1)

            def round_early(s, word):
                round_chunks(s, word, AT_A, (0,))
                round_chunks(s, word, AT_B, (3,))

            def round_late(s, word):
                round_chunks(s, word, AT_A, (1, 2))
                round_chunks(s, word, AT_B, (4, 5))

            def weigh(s, s_plus_1):
                act.wait_ge(zb_ready, s_plus_1)
                nc.scalar.mul(zw[:], zb[:], share_of[:, bass.ds(s, 1)]).then_inc(zw_ready, 1)

            act.wait_ge(s_route, 1)
            act.wait_ge(s_meta, 1)
            zero, one = 0, 1
            copy_xT(1)
            sigmoid(1)
            act.wait_ge(lin_made, 1)
            copy_xT(2)
            word = word_of(act, zero)
            round_chunks(zero, word, AT_A, (0, 1, 2))
            round_chunks(zero, word, AT_B, (3, 4, 5))
            word = word_of(act, one)
            copy_yT(1)
            sigmoid(2)
            round_early(one, word)
            act.wait_ge(lin_made, 2)
            copy_xT(3)
            round_late(one, word)
            weigh(0, 1)
            with act.Fori(2, SLOTS) as s:
                word = word_of(act, s)
                with act.If(bits(act, word, AT_LIVE, 1)):
                    act.wait_ge(z_made, s - 1)
                    copy_yT(s)
                    sigmoid(s + 1)
                    round_early(s, word)
                    act.wait_ge(lin_made, s + 1)
                    copy_xT(s + 2)
                    round_late(s, word)
                    act.wait_ge(scattered, s * 16 - 16)
                    weigh(s - 1, s)
            n_slots = slots_in_use(act)
            act.wait_ge(z_made, n_slots - 1)
            copy_yT(n_slots)
            act.wait_ge(scattered, n_slots * 16 - 16)
            weigh(n_slots - 1, n_slots)

        @block.tensor
        def _(pe):
            pe.wait_ge(s_const, 1)
            pe.wait_ge(s_gws, 3)

            def turn(i):
                pe.wait_ge(s_x[i // TX], 16)
                if i >= NPT:
                    pe.wait_ge(s_lo, i - NPT + 1)
                for k in range(K):
                    last = nc.tensor.transpose(ps_turn[i % NPT][:, k * P:(k + 1) * P], x_sb[:, i, k * P:(k + 1) * P], ident[:])
                last.then_inc(s_turn, 1)

            def gate(i):
                pe.wait_ge(s_lo, i + 1)
                at = i * 2 * E
                for k in range(K):
                    part = slice(k * P, (k + 1) * P)
                    nc.tensor.matmul(ps_gate[:, at:at + 2 * E], x_hi[:, i % NPT, part],
                                     gw_split[:, k, :, :].rearrange("p a e -> p (a e)"), start=(k == 0), stop=False)
                    last = nc.tensor.matmul(ps_gate[:, at:at + E], x_lo[:, i % NPT, part], gw_split[:, k, 0, :],
                                            start=False, stop=(k == K - 1))
                last.then_inc(s_gx, 1)

            for i in range(NT + 2):
                if i < NT:
                    turn(i)
                if i >= 2:
                    gate(i - 2)
            pe.wait_ge(s_wd, 32)
            pe.wait_ge(s_xg8, 1)
            for i in range(NT):
                last = nc.tensor.matmul(ps_log[:, i * E:(i + 1) * E], w_diag[:, i, :], xg8[:, i, :], start=True, stop=True)
            last.then_inc(s_log, 1)

            def condition(i):
                if i >= 2:
                    pe.wait_ge(s_x0c, i - 1)
                nc.tensor.matmul(ps_x0[i % 2][:], w_diag[:, i, :], x_sb[:, i, :], start=True, stop=True).then_inc(s_x0, 1)

            def ranks():
                pe.wait_ge(s_mask, 1)
                nc.tensor.matmul(ps_rank[:], before[:], mask[:].rearrange("p n e -> p (n e)"), start=True, stop=False)
                for j in range(NT):
                    last = nc.tensor.matmul(ps_rank[:, (j + 1) * E:].rearrange("p (n e) -> p n e", e=E), ones[:],
                                            mask[:, j:j + 1, :].to_broadcast([P, NT - j, E]), start=False, stop=(j == NT - 1))
                last.then_inc(s_rank, 1)

            for i in range(NT):
                if i == RANK_AT:
                    ranks()
                condition(i)
            for c in range(2):
                pe.wait_ge(s_row_hot, c + 1)
                pe.wait_ge([s_hot, s_hot2][c], 1)
                for j in range(c * NT, (c + 1) * NT):
                    last = nc.tensor.matmul(ps_tab[:, 0:3 * NS], row_hot[:, j, :],
                                            slot_values[:, j, :, :].rearrange("p a s -> p (a s)"),
                                            start=(j == 0), stop=(j == NP - 1))
            last.then_inc(s_tab, 1)

            def turn_x(rows16):
                pe.wait_ge(gathered, rows16)
                for k in range(K):
                    last = nc.tensor.transpose(ps_xT[:, k * P:(k + 1) * P], xg[:, k * P:(k + 1) * P], ident[:])
                last.then_inc(xT_made, 1)

            def turn_y(s_plus_1):
                pe.wait_ge(y_ready, s_plus_1)
                for k in range(K):
                    last = nc.tensor.transpose(ps_yT[:, k * P:(k + 1) * P], y[:, k * P:(k + 1) * P], ident[:])
                last.then_inc(yT_made, 1)

            def product(dst, hi, lo, w_at, at, done):
                for k in range(K):
                    part = slice(k * P, (k + 1) * P)
                    w_hi = W[:, bass.ds(w_at + (at + k * I), I)]
                    w_lo = W[:, bass.ds(w_at + (WLEN + at + k * I), I)]
                    nc.tensor.matmul(dst[:], hi[:, part], w_hi, start=(k == 0), stop=False)
                    nc.tensor.matmul(dst[:], hi[:, part], w_lo, start=False, stop=False)
                    last = nc.tensor.matmul(dst[:], lo[:, part], w_hi, start=False, stop=(k == K - 1))
                last.then_inc(done, 1)

            def glu_ready(e):
                pe.wait_ge(split_dve, e * 4 + (DVE_START - 2))

            def lin_ready(e):
                pe.wait_ge(split_dve, e * 4 + DVE_START)

            def down_ready(e):
                pe.wait_ge(split_pool, e * 2 + 2)

            turn_x(16)
            pe.wait_ge(s_meta, 1)
            pe.wait_ge(split_pool, 2)
            w_at = 0
            pe.wait_ge(xT_ready, 1)
            product(ps_glu, xT_hi, xT_lo, w_at, GLU, glu_made)
            product(ps_lin, xT_hi, xT_lo, w_at, LIN, lin_made)
            turn_x(32)
            e = expert(pe, word_of(pe, 1))
            w_at, last_at = place_of_w(pe, e), 0
            glu_ready(e)
            pe.wait_ge(xT_ready, 2)
            pe.wait_ge(g_ready, 1)
            product(ps_glu, xT_hi, xT_lo, w_at, GLU, glu_made)
            turn_y(1)
            lin_ready(e)
            product(ps_lin, xT_hi, xT_lo, w_at, LIN, lin_made)
            turn_x(48)
            pe.wait_ge(yT_ready, 1)
            product(ps_z, yT_hi, yT_lo, last_at, DOWN, z_made)
            next_word = pe.alloc_register("next_word")
            pe.reg_load(next_word, meta[0:1, 2:3])
            with pe.Fori(2, SLOTS) as s:
                word = pe.snap(next_word, min_val=0, max_val=(E << AT_BEFORE) - 1)
                with pe.If(bits(pe, word, AT_LIVE, 1)):
                    e, before_e = expert(pe, word), expert_before(pe, word)
                    w_at, last_at = place_of_w(pe, e), place_of_w(pe, before_e)
                    glu_ready(e)
                    pe.wait_ge(xT_ready, s + 1)
                    pe.wait_ge(g_ready, s)
                    product(ps_glu, xT_hi, xT_lo, w_at, GLU, glu_made)
                    turn_y(s)
                    lin_ready(e)
                    product(ps_lin, xT_hi, xT_lo, w_at, LIN, lin_made)
                    turn_x(s * 16 + 32)
                    pe.reg_load(next_word, meta[0:1, bass.ds(s + 1, 1)])
                    down_ready(before_e)
                    pe.wait_ge(yT_ready, s)
                    pe.wait_ge(zb_ready, s - 1)
                    product(ps_z, yT_hi, yT_lo, last_at, DOWN, z_made)
            n_slots = slots_in_use(pe)
            e = expert_before(pe, word_of(pe, n_slots))
            last_at = place_of_w(pe, e)
            turn_y(n_slots)
            down_ready(e)
            pe.wait_ge(yT_ready, n_slots)
            pe.wait_ge(zb_ready, n_slots - 1)
            product(ps_z, yT_hi, yT_lo, last_at, DOWN, z_made)

        @block.vector
        def _(dve):
            v = nc.vector
            chain = [0]

            def link(ins):
                chain[0] += 1
                ins.then_inc(s_dve, 1)
                dve.wait_ge(s_dve, chain[0])

            dve.wait_ge(s_gate, 32)
            v.tensor_copy(gw_split[:, :, 0, :], gw[:]).then_inc(s_gws, 1)
            dve.wait_ge(s_gws, 1)
            v.tensor_tensor(gw_split[:, :, 1, :], gw[:], gw_split[:, :, 0, :].bitcast(F32), ALU.subtract).then_inc(s_gws, 1)
            link(v.memset(mask[:, NT, :], 0.0))
            v.memset(tiles_of[:], 0.0).then_inc(s_gws, 1)
            for i in range(NT):
                dve.wait_ge(s_hi, i + 1)
                if i >= NPT:
                    dve.wait_ge(s_gx, i - NPT + 1)
                v.tensor_tensor(x_lo[:, i % NPT, :], ps_turn[i % NPT][:], x_hi[:, i % NPT, :].bitcast(F32),
                                ALU.subtract).then_inc(s_lo, 1)
            dve.wait_ge(s_gx, NT)
            link(v.tensor_copy(gated_x[:].rearrange("p n a e -> p (n a e)"), ps_gate[:]))
            v.tensor_tensor(xg8[:], gated_x[:, :, 0, :], gated_x[:, :, 1, :], ALU.add).then_inc(s_xg8, 1)

            dve.wait_ge(s_log, 1)
            dve.wait_ge(s_const, N_CONST - 3)
            te = [P, NT, E]
            link(v.tensor_tensor(logits[:], ps_log[:].rearrange("p (n e) -> p n e", e=E),
                                 gb[:].unsqueeze(1).to_broadcast(te), ALU.add))
            rev = rev_id[:].unsqueeze(1).to_broadcast(te)
            src = logits
            for c in range(2):
                link(v.tensor_reduce(best[:, c, :], src[:], AX_X, ALU.max))
                link(v.tensor_tensor(hit[:], src[:], best[:, c, :].unsqueeze(2).to_broadcast(te), ALU.is_equal))
                link(v.tensor_tensor(key[:], hit[:], rev, ALU.mult))
                link(v.tensor_reduce(pick[:, c, :], key[:], AX_X, ALU.max))
                link(v.tensor_tensor(chosen[:, c, :, :], rev, pick[:, c, :].unsqueeze(2).to_broadcast(te), ALU.is_equal))
                if c == 0:
                    link(v.scalar_tensor_tensor(out=rest[:], in0=chosen[:, 0, :, :], scalar=FLOOR, in1=logits[:],
                                                op0=ALU.mult, op1=ALU.add))
                    src = rest
            v.tensor_tensor(mask[:, 0:NT, :], chosen[:, 0, :, :], chosen[:, 1, :, :], ALU.add).then_inc(s_mask, 1)
            v.tensor_tensor(gap[:], best[:, 1, :], best[:, 0, :], ALU.subtract).then_inc(s_gap, 1)
            dve.wait_ge(s_rank, 1)
            een = [P, E, NT]
            link(v.tensor_tensor(full[:], ps_rank[:, NT * E:].unsqueeze(2).to_broadcast(een),
                                 fill_id[:].unsqueeze(1).to_broadcast(een), ALU.is_gt))
            link(v.tensor_reduce(tiles_of[:], full[:], AX_X, ALU.add))
            link(v.tensor_scalar(tiles_of[:], tiles_of[:], 1.0, None, ALU.max))
            link(v.tensor_tensor(bef[:], earlier[:], tiles_of[:].unsqueeze(1).to_broadcast([P, E, E]), ALU.mult))
            link(v.tensor_reduce(base[:], bef[:], AX_X, ALU.add))
            link(v.tensor_scalar(base_rows[:], base[:], float(P), None, ALU.mult))
            link(v.tensor_tensor(place_e[:], ps_rank[:, 0:NT * E].rearrange("p (n e) -> p n e", e=E),
                                 base_rows[:].unsqueeze(1).to_broadcast(te), ALU.add))
            link(v.tensor_tensor(place_k[:], chosen[:], place_e[:].unsqueeze(1).to_broadcast([P, 2, NT, E]), ALU.mult))
            link(v.tensor_reduce(place[:], place_k[:].rearrange("p c n e -> p (c n) e"), AX_X, ALU.add))
            link(v.tensor_copy(place_i[:], place[:]))
            link(v.tensor_scalar(row_of[:], place_i[:], P - 1, None, ALU.bitwise_and))
            link(v.tensor_scalar(slot_of[:], place_i[:], P.bit_length() - 1, None, ALU.arith_shift_right))
            dve.wait_ge(s_egap, 1)
            link(v.tensor_scalar(den[:], egap[:], 1.0, None, ALU.add))
            link(v.reciprocal(share[:, 0:NT], den[:]))
            link(v.tensor_tensor(share[:, NT:NP], share[:, 0:NT], egap[:], ALU.mult))
            link(v.tensor_copy(share_hi[:], share[:]))
            link(v.tensor_copy(values[:, :, 1], share_hi[:].bitcast(F32)))
            link(v.tensor_tensor(values[:, :, 2], share[:], share_hi[:].bitcast(F32), ALU.subtract))
            v.tensor_tensor(slot_hot[:], slot_of[:].unsqueeze(2).to_broadcast([P, NP, NS]),
                            slot_id[:].unsqueeze(1).to_broadcast([P, NP, NS]), ALU.is_equal).then_inc(s_slot_hot, 1)
            dve.wait_ge(s_slot_hot, 1)
            spread_values(v, 0).then_inc(s_hot, 1)
            dve.wait_ge(s_wr, 16)
            for c in range(2):
                h = slice(c * NT, (c + 1) * NT)
                v.tensor_tensor(row_hot[:, h, :], row_of[:, h].unsqueeze(2).to_broadcast([P, NT, P]),
                                row_id[:].unsqueeze(1).to_broadcast([P, NT, P]), ALU.is_equal).then_inc(s_row_hot, 1)
            ese = [1, NS, E]
            link(v.tensor_tensor(ends[:], base[0:1, :], tiles_of[0:1, :], ALU.add))
            link(v.tensor_scalar(extra_i[:], ends[:, E - 1:E], float(-NT), None, ALU.add))
            link(v.tensor_tensor(over[:], slot_id[0:1, :].unsqueeze(2).to_broadcast(ese),
                                 ends[:].unsqueeze(1).to_broadcast(ese), ALU.is_ge))
            link(v.tensor_reduce(ended[:], over[:], AX_X, ALU.add))
            link(v.tensor_scalar(expert_of[:], ended[:], float(E - 1), None, ALU.min))
            v.tensor_scalar(live[:], ended[:], float(E), None, ALU.is_lt)
            link(v.tensor_tensor(over[:], over[:], ends[:].unsqueeze(1).to_broadcast(ese), ALU.mult))
            link(v.tensor_reduce(first_of[:], over[:], AX_X, ALU.max))
            link(v.tensor_scalar(first_of[:], first_of[:], 1.0, None, ALU.max))
            link(v.scalar_tensor_tensor(out=packed[:], in0=live[:], scalar=float(1 << AT_LIVE), in1=expert_of[:],
                                        op0=ALU.mult, op1=ALU.add))
            link(v.scalar_tensor_tensor(out=packed[:], in0=first_of[:], scalar=float(1 << AT_FIRST), in1=packed[:],
                                        op0=ALU.mult, op1=ALU.add))
            link(v.scalar_tensor_tensor(out=packed[:, 1:], in0=expert_of[:, 0:NS - 1], scalar=float(1 << AT_BEFORE),
                                        in1=packed[:, 1:], op0=ALU.mult, op1=ALU.add))
            dve.wait_ge(s_tab, 1)
            link(v.tensor_copy(table[:].rearrange("p a s -> p (a s)"), ps_tab[:, 0:3 * NS]))
            link(v.tensor_scalar(fill[:], table[:, 0, :], 0.0, pad_id[:, 0:1], ALU.is_equal, ALU.mult))
            v.tensor_tensor(share_of[:], table[:, 1, :], table[:, 2, :], ALU.add)
            v.scalar_tensor_tensor(out=tokens[:], in0=table[:, 0, :], scalar=-1.0, in1=fill[:],
                                   op0=ALU.add, op1=ALU.add).then_inc(s_route, 1)

            link(v.tensor_scalar(lasts[:], ends[:], -1.0, None, ALU.add))
            link(v.tensor_scalar(turn_a[:], ends[:], -2.0, None, ALU.add))
            link(v.tensor_tensor(turn_a[:], turn_a[:], base[0:1, :], ALU.max))
            link(v.tensor_scalar(turn_b[:], base[0:1, :], 1.0, None, ALU.add))
            link(v.tensor_tensor(turn_a[:], turn_a[:], turn_b[:], ALU.min))
            link(v.tensor_scalar(turn_b[:], base[0:1, :], 2.0, None, ALU.add))
            link(v.tensor_tensor(turn_b[:], turn_b[:], lasts[:], ALU.min))
            esf = [1, NS, E - 1]
            for half, turn_of, at in ((0, turn_a, AT_A), (1, turn_b, AT_B)):
                link(v.tensor_tensor(at_turn[:], slot_id[0:1, :].unsqueeze(2).to_broadcast(esf),
                                     turn_of[:, 0:E - 1].unsqueeze(1).to_broadcast(esf), ALU.is_equal))
                link(v.tensor_reduce(splits[:, half, :], at_turn[:], AX_X, ALU.max))
                link(v.scalar_tensor_tensor(out=[packed, meta][half][:], in0=splits[:, half, :], scalar=float(1 << at),
                                            in1=packed[:], op0=ALU.mult, op1=ALU.add))
            v.memset(turn_a[:], 0.0).then_inc(s_meta, 1)
            v.memset(turn_b[:], 0.0).then_inc(split_dve, DVE_START)

            def glu(b_at, s_plus_1):
                dve.wait_ge(glu_made, s_plus_1)
                v.tensor_tensor(g[:], ps_glu[:], BI[:, bass.ds(b_at + BG, I)], ALU.add).then_inc(g_ready, 1)

            def linear(b_at, s_plus_1):
                dve.wait_ge(lin_made, s_plus_1)
                v.tensor_tensor(lin[:], ps_lin[:], BI[:, bass.ds(b_at + BL, I)], ALU.add).then_inc(part_ready, 1)

            def gate_g(s_plus_1):
                dve.wait_ge(sig_ready, s_plus_1)
                v.tensor_tensor(gs[:], g[:], sig[:], ALU.mult).then_inc(part_ready, 1)

            def join(parts):
                dve.wait_ge(part_ready, parts)
                v.scalar_tensor_tensor(out=y[:], in0=lin[:], scalar=1.0, in1=gs[:],
                                       op0=ALU.add, op1=ALU.mult).then_inc(y_ready, 1)

            def low_xT(s_plus_1):
                dve.wait_ge(xT_rounded, s_plus_1)
                v.tensor_tensor(xT_lo[:], ps_xT[:], xT_hi[:].bitcast(F32), ALU.subtract).then_inc(xT_ready, 1)

            def low_yT(s_plus_1):
                dve.wait_ge(yT_rounded, s_plus_1)
                v.tensor_tensor(yT_lo[:], ps_yT[:], yT_hi[:].bitcast(F32), ALU.subtract).then_inc(yT_ready, 1)

            def down(b_at, s_plus_1):
                dve.wait_ge(z_made, s_plus_1)
                v.tensor_tensor(zb[:], ps_z[:], BI[:, bass.ds(b_at + BD, H)], ALU.add).then_inc(zb_ready, 1)

            def low_chunks(word, flag, chunks):
                with dve.If(bits(dve, word, flag, 1)):
                    e = expert(dve, word)
                    to = next_place_of_w(dve, e)
                    for c in chunks:
                        dve.wait_ge(split_hi, e * CHUNKS + (CHUNKS + c + 1))
                        v.tensor_tensor(W[:, bass.ds(to + (WLEN + c * PIECE), PIECE)], raw[:, c * PIECE:(c + 1) * PIECE],
                                        W[:, bass.ds(to + c * PIECE, PIECE)].bitcast(F32), ALU.subtract).then_inc(split_dve, 1)

            low_xT(1)
            dve.wait_ge(s_meta, 1)
            word = word_of(dve, 0)
            b_at = 0
            glu(b_at, 1)
            linear(b_at, 1)
            low_xT(2)
            gate_g(1)
            join(2)
            low_chunks(word, AT_A, (0, 1))
            low_chunks(word, AT_B, (2, 3))
            word = word_of(dve, 1)
            b_at, last_at = place_of_b(dve, expert(dve, word)), 0
            glu(b_at, 2)
            low_yT(1)
            linear(b_at, 2)
            low_xT(3)
            gate_g(2)
            join(4)
            down(last_at, 1)
            low_chunks(word, AT_A, (0, 1))
            low_chunks(word, AT_B, (2, 3))
            with dve.Fori(2, SLOTS) as s:
                word = word_of(dve, s)
                with dve.If(bits(dve, word, AT_LIVE, 1)):
                    b_at = place_of_b(dve, expert(dve, word))
                    last_at = place_of_b(dve, expert_before(dve, word))
                    glu(b_at, s + 1)
                    low_yT(s)
                    linear(b_at, s + 1)
                    low_xT(s + 2)
                    gate_g(s + 1)
                    join(s * 2 + 2)
                    dve.wait_ge(zw_ready, s - 1)
                    down(last_at, s)
                    low_chunks(word, AT_A, (0, 1))
                    low_chunks(word, AT_B, (2, 3))
            n_slots = slots_in_use(dve)
            last_at = place_of_b(dve, expert_before(dve, word_of(dve, n_slots)))
            low_yT(n_slots)
            dve.wait_ge(zw_ready, n_slots - 1)
            down(last_at, n_slots)


def kernel(x, itok_B_1_198, L0_cond_weights, L0_ffn_gate_w, L0_ffn_gate_b, L0_ffn_w1, L0_ffn_b1, L0_ffn_w2, L0_ffn_b2):
    import numpy as np
    import concourse.bacc as bacc
    from concourse.bass_utils import run_bass_kernel_spmd

    B, C, H = x.shape
    E = L0_ffn_w1.shape[0]
    K = H // P

    def by_rows(w):
        w = np.asarray(w)
        return w.transpose(0, 2, 1).reshape(E, K, P, w.shape[1]).transpose(0, 2, 1, 3).reshape(E, P, K * w.shape[1])

    w1, b1 = np.asarray(L0_ffn_w1), np.asarray(L0_ffn_b1)
    arrays = {
        "x": np.asarray(x).reshape(B * C, H),
        "cond": np.asarray(itok_B_1_198).reshape(B, 1),
        "cond_w": np.asarray(L0_cond_weights),
        "gate_w": np.asarray(L0_ffn_gate_w).T.reshape(K, P, E).transpose(1, 0, 2),
        "gate_b": np.asarray(L0_ffn_gate_b),
        "ffn_w": np.concatenate([by_rows(w1[:, 0::2]), by_rows(w1[:, 1::2]), by_rows(L0_ffn_w2)], axis=2),
        "ffn_b": np.concatenate([b1[:, 0::2], b1[:, 1::2], np.asarray(L0_ffn_b2)], axis=1),
    }
    arrays = {k: np.ascontiguousarray(a) for k, a in arrays.items()}
    nc = bacc.Bacc("TRN2", target_bir_lowering=False, num_devices=1)
    ins = [nc.dram_tensor(n, a.shape, mybir.dt.from_np(a.dtype), kind="ExternalInput").ap() for n, a in arrays.items()]
    cond_rows = nc.dram_tensor("cond_rows", (B, C * C), F32, kind="Internal").ap()
    x0_rows = nc.dram_tensor("x0_rows", (B * C + P, H), F32, kind="Internal").ap()
    out = nc.dram_tensor("out", (B * C + P, H), F32, kind="ExternalOutput").ap()
    adaln_moe_kernel(nc, *ins, cond_rows, x0_rows, out)
    r = run_bass_kernel_spmd(nc, [arrays], core_ids=[0])
    return r.results[0]["out"][:B * C].reshape(B, C, H)
```

```python
from contextlib import ExitStack

import concourse.bass as bass
from concourse import mybir

P = 128
ALU = mybir.AluOpType
ACT = mybir.ActivationFunctionType
F32 = mybir.dt.float32
F32R = mybir.dt.float32r
BF16 = mybir.dt.bfloat16
I32 = mybir.dt.int32
AX_X = mybir.AxisListType.X

RING = 2
B_RING = 3
CHUNKS = 6
FLOOR = -3.0e38


def adaln_moe_kernel(nc, x, cond, cond_w, gate_w, gate_b, ffn_w, ffn_b, cond_rows, x0_rows, out):
    TOKENS, H = x.shape
    B = cond.shape[0]
    C = TOKENS // B
    E = ffn_w.shape[0]
    K = H // P
    I = H
    NT = TOKENS // P
    SLOTS = (2 * TOKENS + E * (P - 1)) // P
    NS = SLOTS + 1
    NP = 2 * NT
    GLU, LIN, DOWN = 0, K * I, 2 * K * I
    WLEN = 2 * K * I + K * H
    BG, BL, BD = 0, I, 2 * I
    BLEN = 2 * I + H
    NX = 8
    TX = NT // NX
    NG = 8
    TG = NT // NG
    X0_RING = 12
    NO = 4
    TO = NT // NO
    EARLY = 2
    AMONG = 2
    RANK_AT = 5
    GROUP = 4
    NXT = 2 * GROUP
    HALF = CHUNKS // 2
    PIECE = WLEN // CHUNKS
    A_LOADS = 16 * HALF
    B_LOADS = 16 * HALF + 16
    E_BITS, S_BITS = (E - 1).bit_length(), SLOTS.bit_length()
    AT_A = E_BITS
    AT_B = AT_A + 1
    AT_LIVE = AT_B + 1
    AT_END = AT_LIVE + 1
    AT_FIRST = AT_END + 1
    AT_BEFORE = AT_FIRST + S_BITS
    DVE_START = 3
    assert B == 2 * NT and C == 64 and ffn_w.shape[2] == WLEN and ffn_b.shape[1] == BLEN

    with ExitStack() as ctx:
        def sb(name, shape, dt=F32):
            return ctx.enter_context(nc.sbuf_tensor(name, shape, dt))

        def psum(name, shape):
            return ctx.enter_context(nc.psum_tensor(name, shape, F32))

        def sem(name):
            return ctx.enter_context(nc.semaphore(name))

        ident = sb("ident", [P, P])
        before = sb("before", [P, P], BF16)
        ones = sb("ones", [P, P], BF16)
        row_id = sb("row_id", [P, P])
        slot_id = sb("slot_id", [P, NS])
        rev_id = sb("rev_id", [P, E])
        fill_id = sb("fill_id", [P, NT])
        earlier = sb("earlier", [P, E, E])
        pad_id = sb("pad_id", [P, 1])
        cond_sb = sb("cond_sb", [B, 1], I32)
        w_diag = sb("w_diag", [P, NT, P])
        gw = sb("gw", [P, K, E])
        gw_split = sb("gw_split", [P, K, 2, E], F32R)
        gb = sb("gb", [P, E])
        gated = sb("gated", [P, NT, 2, E])
        xg8 = sb("xg8", [P, NT, E])
        logits = sb("logits", [P, NT, E])
        rest = sb("rest", [P, NT, E])
        hit = sb("hit", [P, NT, E])
        key = sb("key", [P, NT, E])
        best = sb("best", [P, 2, NT])
        pick = sb("pick", [P, 2, NT])
        chosen = sb("chosen", [P, 2, NT, E])
        gap = sb("gap", [P, NT])
        egap = sb("egap", [P, NT])
        den = sb("den", [P, NT])
        table_loader = sb("table_loader", [P, NT])
        share = sb("share", [P, NP])
        share_hi = sb("share_hi", [P, NP], F32R)
        mask = sb("mask", [P, NT + 1, E], BF16)
        full = sb("full", [P, E, NT])
        tiles_of = sb("tiles_of", [P, E])
        bef = sb("bef", [P, E, E])
        base = sb("base", [P, E])
        base_rows = sb("base_rows", [P, E])
        place_e = sb("place_e", [P, NT, E])
        place_k = sb("place_k", [P, 2, NT, E])
        place = sb("place", [P, NP])
        place_i = sb("place_i", [P, NP], I32)
        slot_of = sb("slot_of", [P, NP], I32)
        row_of = sb("row_of", [P, NP], I32)
        values = sb("values", [P, NP, 3])
        slot_hot = sb("slot_hot", [P, NP, NS])
        with ExitStack() as early:
            cond_mats = early.enter_context(nc.sbuf_tensor("cond_mats", [B, C * C], F32))
        row_hot = sb("row_hot", [P, NP, P], F32R)
        table = sb("table", [P, 3, NS])
        fill = sb("fill", [P, NS])
        tokens = sb("tokens", [P, NS], I32)
        share_of = sb("share_of", [P, NS])
        ends = sb("ends", [1, E])
        over = sb("over", [1, NS, E])
        ended = sb("ended", [1, NS])
        expert_of = sb("expert_of", [1, NS])
        splits = sb("splits", [1, 2, NS])
        lasts = sb("lasts", [1, E])
        turn_a = sb("turn_a", [1, E])
        turn_b = sb("turn_b", [1, E])
        at_turn = sb("at_turn", [1, NS, E - 1])
        meta = sb("meta", [1, NS + 1], I32)
        packed = sb("packed", [1, NS])
        live = sb("live", [1, NS])
        at_end = sb("at_end", [1, NS])
        first_of = sb("first_of", [1, NS])
        BI = sb("BI", [P, B_RING * BLEN])
        raw = sb("raw", [P, WLEN])
        with ExitStack() as early:
            early.enter_context(nc.sbuf_tensor("first_half", [P, 2 * WLEN], F32))
            x_sb = early.enter_context(nc.sbuf_tensor("x_sb", [P, NT, H], F32))
            with ExitStack() as first:
                gated_x = first.enter_context(nc.sbuf_tensor("gated_x", [2 * E, NT * P], F32))
            slot_values = early.enter_context(nc.sbuf_tensor("slot_values", [P, NP, 3, NS], F32R))
        W = sb("W", [P, RING * 2 * WLEN], F32R)
        x_hi = W[:, 0:NXT * H].rearrange("p (n h) -> p n h", h=H)
        x_lo = W[:, NXT * H:2 * NXT * H].rearrange("p (n h) -> p n h", h=H)
        with ExitStack() as early:
            x0_sb = early.enter_context(nc.sbuf_tensor("x0_sb", [P, X0_RING, H], F32))
        xg = sb("xg", [P, H])
        xT_hi = sb("xT_hi", [P, K * P], F32R)
        xT_lo = sb("xT_lo", [P, K * P], F32R)
        g = sb("g", [P, I])
        lin = sb("lin", [P, I])
        sig = sb("sig", [P, I])
        gs = sb("gs", [P, I])
        y = sb("y", [P, I])
        yT_hi = sb("yT_hi", [P, K * P], F32R)
        yT_lo = sb("yT_lo", [P, K * P], F32R)
        zb = sb("zb", [P, H])
        zw = sb("zw", [P, H])
        gather_at = sb("gather_at", [P, 1], I32)
        scatter_at = sb("scatter_at", [P, 1], I32)

        ps_glu = psum("ps_glu", [P, I])
        ps_lin = psum("ps_lin", [P, I])
        ps_z = psum("ps_z", [P, H])
        ps_xT = psum("ps_xT", [P, K * P])
        ps_yT = psum("ps_yT", [P, K * P])
        ps_gate = psum("ps_gate", [P, max(NT * 2 * E, 3 * NS)])
        ps_rank = psum("ps_rank", [P, (NT + 1) * E])
        ps_log = psum("ps_log", [P, NT * E])
        ps_x0 = [ps_glu, ps_lin]
        ps_turn = [ps_xT, ps_yT, ps_z]
        ps_gated = [ps_glu, ps_lin]
        ps_tab = ps_gate
        NPS = len(ps_turn)

        s_cond = sem("s_cond")
        s_gate = sem("s_gate")
        s_x = [sem(f"s_x_part{n}") for n in range(NX)]
        s_wz = sem("s_wz")
        s_wg = sem("s_wg")
        s_wr = sem("s_wr")
        s_wd = sem("s_wd")
        s_const = sem("s_const")
        s_gws = sem("s_gws")
        s_turn = sem("s_turn")
        s_hi = sem("s_hi")
        s_lo = sem("s_lo")
        s_gx = sem("s_gx")
        s_gated = sem("s_gated")
        s_back = sem("s_back")
        s_xg8 = sem("s_xg8")
        s_x0 = sem("s_x0")
        s_x0c = sem("s_x0c")
        s_log = sem("s_log")
        s_rows = [sem(f"s_rows{n}") for n in range(NG)]
        s_pad = sem("s_pad")
        s_init = sem("s_init")
        s_gap = sem("s_gap")
        s_egap = sem("s_egap")
        s_mask = sem("s_mask")
        s_rank = sem("s_rank")
        s_slot_hot = sem("s_slot_hot")
        s_row_hot = sem("s_row_hot")
        s_hot = sem("s_hot")
        s_hot2 = sem("s_hot2")
        s_tab = sem("s_tab")
        s_route = sem("s_route")
        s_meta = sem("s_meta")
        s_dve = sem("s_dve")
        s_pool = sem("s_pool")
        loaded_a = sem("loaded_a")
        loaded_b = sem("loaded_b")
        gathered = sem("gathered")
        xT_made = sem("xT_made")
        xT_rounded = sem("xT_rounded")
        xT_ready = sem("xT_ready")
        split_hi = [sem("split_hi_a"), sem("split_hi_b")]
        split_dve = sem("split_dve")
        split_pool = sem("split_pool")
        glu_made = sem("glu_made")
        lin_made = sem("lin_made")
        g_ready = sem("g_ready")
        sig_ready = sem("sig_ready")
        part_ready = sem("part_ready")
        y_ready = sem("y_ready")
        yT_made = sem("yT_made")
        yT_rounded = sem("yT_rounded")
        yT_ready = sem("yT_ready")
        z_made = sem("z_made")
        zb_ready = sem("zb_ready")
        zw_ready = sem("zw_ready")
        scattered = sem("scattered")
        s_last = sem("s_last")
        at_ready = sem("at_ready")
        turns = sem("turns")

        x_t = x.rearrange("(n p) h -> p n h", p=P)
        x0_t = x0_rows[0:TOKENS, :].rearrange("(n p) h -> p n h", p=P)
        out_t = out[0:TOKENS, :].rearrange("(n p) h -> p n h", p=P)
        w_parts = ffn_w.rearrange("e p (c n) -> e p c n", c=CHUNKS)
        raw_parts = raw[:].rearrange("p (c n) -> p c n", c=CHUNKS)
        pairs = cond_rows.rearrange("(n two) (c d) -> two c n d", two=2, d=C)
        N_CONST = 12
        INITS = 16 * (NO + 1)

        def word_of(eng, s):
            return eng.value_load(meta[0:1, bass.ds(s, 1)], min_val=0, max_val=(E << AT_BEFORE) - 1)

        def as_word(eng, register):
            return eng.snap(register, min_val=0, max_val=(E << AT_BEFORE) - 1)

        def bits(eng, word, at, n):
            return eng.snap((word >> at) & ((1 << n) - 1), min_val=0, max_val=(1 << n) - 1)

        def expert(eng, word):
            return bits(eng, word, 0, E_BITS)

        def expert_before(eng, word):
            return bits(eng, word, AT_BEFORE, E_BITS)

        def place_of_w(eng, e):
            return eng.snap((e & (RING - 1)) * (2 * WLEN), min_val=0, max_val=(RING - 1) * 2 * WLEN)

        def next_place_of_w(eng, e):
            return eng.snap(((e + 1) & (RING - 1)) * (2 * WLEN), min_val=0, max_val=(RING - 1) * 2 * WLEN)

        def place_of_b(eng, e):
            return eng.snap((e % B_RING) * BLEN, min_val=0, max_val=(B_RING - 1) * BLEN)

        def spread_values(eng, c):
            h = slice(c * NT, (c + 1) * NT)
            nas = [P, NT, 3, NS]
            return eng.tensor_tensor(slot_values[:, h, :, :], slot_hot[:, h, :].unsqueeze(2).to_broadcast(nas),
                                     values[:, h, :].unsqueeze(3).to_broadcast(nas), ALU.mult)

        block = ctx.enter_context(nc.Block())

        @block.sync
        def _(sp):
            sp.dma_start(cond_sb[:], cond).then_inc(s_cond, 16)

            def load_x(n):
                sp.dma_start(x_sb[:, n * TX:(n + 1) * TX, :], x_t[:, n * TX:(n + 1) * TX, :]).then_inc(s_x[n], 16)

            for n in range(NX // 2 + 1):
                load_x(n)
            sp.wait_ge(s_wg, 16)
            sp.dma_start(cond_rows, cond_mats[:]).then_inc(s_wr, 16)
            for n in range(NX // 2 + 1, NX):
                load_x(n)
            sp.wait_ge(s_wr, 16)
            sp.wait_ge(s_wz, 1)
            for half in range(2):
                rows = slice(half * C, (half + 1) * C)
                sp.dma_start(w_diag[rows, :, rows], pairs[half]).then_inc(s_wd, 16)

            def load(e, c):
                half, n, of = [(loaded_a, c, A_LOADS), (loaded_b, c - HALF, B_LOADS)][c // HALF]
                sp.wait_ge(half, e * of + n * 16)
                sp.dma_start(raw_parts[:, c, :], w_parts[e, :, c, :]).then_inc(half, 16)

            def load_biases(e):
                at = (e % B_RING) * BLEN
                sp.wait_ge(loaded_b, e * B_LOADS + B_LOADS - 16)
                sp.dma_start(BI[:, at:at + BLEN], ffn_b[e].partition_broadcast(P)).then_inc(loaded_b, 16)

            for c in range(CHUNKS):
                sp.dma_start(raw_parts[:, c, :], w_parts[0, :, c, :]).then_inc([loaded_a, loaded_b][c // HALF], 16)
            sp.dma_start(BI[:, 0:BLEN], ffn_b[0].partition_broadcast(P)).then_inc(loaded_b, 16)
            for n in range(NX):
                sp.wait_ge(s_x[n], 16)

            def start_out(n):
                sp.dma_start(out_t[:, n * TO:(n + 1) * TO, :], x_sb[:, n * TO:(n + 1) * TO, :]).then_inc(s_init, 16)

            for n in range(NO - 1):
                start_out(n)
            sp.wait_ge(split_pool, 2)
            sp.wait_ge(s_rows[NG - 1], 16)
            load(1, 0)
            load(1, 1)
            sp.wait_ge(gathered, 16)
            start_out(NO - 1)
            sp.dma_start(out[TOKENS:TOKENS + P, :], x_sb[:, 0, :]).then_inc(s_init, 16)
            for e in range(1, E):
                for c in range(CHUNKS):
                    if e == 1:
                        if c < 2:
                            continue
                    elif c < 4:
                        sp.wait_ge(split_dve, DVE_START + 4 * (e - 2) + c + 1)
                    else:
                        sp.wait_ge(split_pool, 2 * (e - 1) + c - 3)
                    load(e, c)
                load_biases(e)
            sp.wait_ge(loaded_a, A_LOADS * E)
            sp.wait_ge(loaded_b, B_LOADS * E)
            sp.wait_ge(s_init, INITS)

        @block.gpsimd
        def _(pool):
            nc.gpsimd.memset(ident[:], 0.0).then_inc(s_pool, 1)
            nc.gpsimd.memset(ones[:], 1.0).then_inc(s_pool, 1)
            nc.gpsimd.memset(earlier[:], 1.0).then_inc(s_pool, 1)
            pool.wait_ge(s_pool, 3)
            nc.gpsimd.affine_select(out=ident[:], in_=ident[:], compare_op=ALU.not_equal, fill=1.0, base=0,
                                    pattern=[[-1, P]], channel_multiplier=1).then_inc(s_const, 1)
            pool.wait_ge(s_cond, 16)
            nc.gpsimd.indirect_dma_start(
                out=cond_mats[:], out_offset=None, in_=cond_w.rearrange("s c d -> s (c d)"),
                in_offset=bass.IndirectOffsetOnAxis(ap=cond_sb[:, 0:1], axis=0)).then_inc(s_wg, 16)
            nc.gpsimd.memset(w_diag[:], 0.0).then_inc(s_wz, 1)
            nc.gpsimd.affine_select(out=before[:], in_=ones[:], compare_op=ALU.is_gt, fill=0.0, base=0,
                                    pattern=[[1, P]], channel_multiplier=-1).then_inc(s_const, 1)
            nc.gpsimd.affine_select(out=earlier[:], in_=earlier[:], compare_op=ALU.is_gt, fill=0.0, base=0,
                                    pattern=[[1, E], [-1, E]], channel_multiplier=0).then_inc(s_const, 1)

            def iota(t, pattern, base=0, mult=0):
                nc.gpsimd.iota(t, pattern=pattern, base=base, channel_multiplier=mult,
                               allow_small_or_imprecise_dtypes=True).then_inc(s_const, 1)

            iota(row_id[:], [[1, P]])
            iota(values[:, :, 0], [[0, 2], [P, NT]], base=1, mult=1)
            iota(slot_id[:], [[1, NS]])
            iota(rev_id[:], [[-1, E]], base=E)
            iota(fill_id[:], [[P, NT]])
            iota(pad_id[:], [[0, 1]], base=TOKENS + 1, mult=1)

            def low_first(c):
                at = c * PIECE
                pool.wait_ge(split_hi[c // HALF], c % HALF + 1)
                return nc.gpsimd.tensor_tensor(W[:, WLEN + at:WLEN + at + PIECE], raw[:, at:at + PIECE],
                                               W[:, at:at + PIECE].bitcast(F32), ALU.subtract)

            for c in range(CHUNKS):
                last = low_first(c)
            last.then_inc(split_pool, 2)
            pool.wait_ge(s_slot_hot, 1)
            spread_values(nc.gpsimd, 1).then_inc(s_hot2, 1)
            pool.wait_ge(s_route, 1)
            for n in range(NG):
                pool.wait_ge(s_rows[n], 16)
            pool.wait_ge(s_pad, 16)

            def gather(s):
                nc.gpsimd.tensor_copy(gather_at[:], tokens[:, bass.ds(s, 1)]).then_inc(at_ready, 1)

            def scatter(s):
                nc.gpsimd.tensor_copy(scatter_at[:], tokens[:, bass.ds(s, 1)]).then_inc(at_ready, 1)

            def start_gather():
                nc.gpsimd.indirect_dma_start(
                    out=xg[:], out_offset=None, in_=x0_rows[:, :],
                    in_offset=bass.IndirectOffsetOnAxis(ap=gather_at[:, 0:1], axis=0)).then_inc(gathered, 16)

            def start_scatter(done):
                nc.gpsimd.indirect_dma_start(
                    out=out[:, :], out_offset=bass.IndirectOffsetOnAxis(ap=scatter_at[:, 0:1], axis=0),
                    in_=zw[:], in_offset=None, compute_op=ALU.add).then_inc(done, 16)

            def split_down(word):
                with pool.If(bits(pool, word, AT_B, 1)):
                    e = expert(pool, word)
                    to = next_place_of_w(pool, e)
                    for c in (4, 5):
                        pool.wait_ge(split_hi[c // HALF], e * HALF + (HALF + c % HALF + 1))
                        nc.gpsimd.tensor_tensor(W[:, bass.ds(to + (WLEN + c * PIECE), PIECE)], raw[:, c * PIECE:(c + 1) * PIECE],
                                                W[:, bass.ds(to + c * PIECE, PIECE)].bitcast(F32),
                                                ALU.subtract).then_inc(split_pool, 1)

            for s in range(3):
                if s > 0:
                    pool.wait_ge(xT_made, s)
                gather(s)
                pool.wait_ge(at_ready, s + 1)
                start_gather()
            pool.wait_ge(s_meta, 1)
            split_down(word_of(pool, 0))
            pool.wait_ge(s_init, INITS)
            next_word = pool.alloc_register("next_word")
            word_back_1 = pool.alloc_register("word_back_1")
            word_back_2 = pool.alloc_register("word_back_2")
            pool.reg_load(next_word, meta[0:1, 3:4])
            pool.reg_load(word_back_1, meta[0:1, 2:3])
            pool.reg_load(word_back_2, meta[0:1, 1:2])
            with pool.Fori(3, NS) as s:
                word, word_2 = as_word(pool, next_word), as_word(pool, word_back_2)
                pool.reg_mov(word_back_2, word_back_1)
                pool.reg_mov(word_back_1, next_word)
                with pool.If(bits(pool, word, AT_LIVE, 1)):
                    pool.wait_ge(xT_made, s)
                    gather(s)
                    pool.wait_ge(at_ready, s * 2 - 2)
                    pool.sem_inc(turns, 1)
                    start_gather()
                    scatter(s - 3)
                    pool.wait_ge(zw_ready, s - 2)
                    pool.wait_ge(at_ready, s * 2 - 1)
                    pool.sem_inc(turns, 1)
                    start_scatter(scattered)
                    pool.reg_load(next_word, meta[0:1, bass.ds(s + 1, 1)])
                    split_down(word_2)
                    pool.wait_ge(scattered, s * 16 - 32)
                with pool.If(bits(pool, word, AT_END, 1)):
                    pool.wait_ge(xT_made, s)
                    gather(s)
                    pool.wait_ge(at_ready, s * 2 - 2)
                    pool.sem_inc(turns, 1)
                    start_gather()
                    pool.reg_mov(next_word, 0)
                    split_down(word_2)
                    for back in (3, 2, 1):
                        scatter(s - back)
                        pool.wait_ge(zw_ready, s + (1 - back))
                        pool.wait_ge(at_ready, s * 2 + (2 - back))
                        pool.sem_inc(turns, 1)
                        start_scatter([scattered, s_last][back == 1])
                        if back > 1:
                            pool.wait_ge(scattered, s * 16 + 16 * (1 - back))
            pool.wait_ge(s_last, 16)

        @block.scalar
        def _(act):
            act.dma_start(gw[:], gate_w).then_inc(s_gate, 16)
            act.dma_start(gb[:], gate_b.partition_broadcast(P)).then_inc(s_gate, 16)
            def copy_gated(g):
                act.wait_ge(s_gx, g + 1)
                nc.scalar.copy(gated_x[:, g * GROUP * P:(g + 1) * GROUP * P], ps_gated[g % 2][0:2 * E, :]).then_inc(s_gated, 1)

            for i in range(NT):
                act.wait_ge(s_turn, i + 1)
                if i >= NXT:
                    act.wait_ge(s_gx, (i - NXT) // GROUP + 1)
                nc.scalar.copy(x_hi[:, i % NXT, :], ps_turn[i % NPS][:]).then_inc(s_hi, 1)
                if i >= 2 * GROUP - 1 and i % GROUP == GROUP - 1:
                    copy_gated(i // GROUP - 1)
            copy_gated(NT // GROUP - 1)
            def exp_gap():
                act.wait_ge(s_gap, 1)
                nc.scalar.activation(egap[:], gap[:], ACT.Exp).then_inc(s_egap, 1)
                nc.scalar.activation(table_loader[:], gap[:], ACT.Sigmoid)

            def round_first(c):
                act.wait_ge([loaded_a, loaded_b][c // HALF], [A_LOADS, B_LOADS][c // HALF])
                nc.scalar.copy(W[:, c * PIECE:(c + 1) * PIECE], raw[:, c * PIECE:(c + 1) * PIECE]).then_inc(split_hi[c // HALF], 1)

            for i in range(NT):
                if i == EARLY:
                    for c in range(HALF):
                        round_first(c)
                    act.dma_start(x0_rows[TOKENS:TOKENS + P, :], x_sb[:, 0, :]).then_inc(s_pad, 16)
                if i == RANK_AT:
                    exp_gap()
                act.wait_ge(s_x0, i + 1)
                if i >= X0_RING and i % TG == 0:
                    act.wait_ge(s_rows[(i - X0_RING) // TG], 16)
                nc.scalar.copy(x0_sb[:, i % X0_RING, :], ps_x0[i % 2][:]).then_inc(s_x0c, 1)
                if EARLY <= i < EARLY + HALF:
                    round_first(i - EARLY + HALF)
                if i % TG == TG - 1:
                    n, at = i // TG, (i // TG) * TG % X0_RING
                    act.wait_ge(s_x0c, i + 1)
                    act.dma_start(x0_t[:, n * TG:(n + 1) * TG, :], x0_sb[:, at:at + TG, :]).then_inc(s_rows[n], 16)

            def copy_xT(s_plus_1):
                act.wait_ge(xT_made, s_plus_1)
                nc.scalar.copy(xT_hi[:], ps_xT[:]).then_inc(xT_rounded, 1)

            def sigmoid(s_plus_1):
                act.wait_ge(g_ready, s_plus_1)
                nc.scalar.activation(sig[:], g[:], ACT.Sigmoid, scale=1.702).then_inc(sig_ready, 1)

            def copy_yT(s_plus_1):
                act.wait_ge(yT_made, s_plus_1)
                nc.scalar.copy(yT_hi[:], ps_yT[:]).then_inc(yT_rounded, 1)

            def round_chunks(s, word, flag, chunks):
                first_slot = isinstance(s, int) and s == 0
                with act.If(bits(act, word, flag, 1)):
                    e = expert(act, word)
                    to = next_place_of_w(act, e)
                    if 0 in chunks:
                        act.wait_ge(loaded_a, e * A_LOADS + 2 * A_LOADS)
                        if not first_slot:
                            act.wait_ge(lin_made, s)
                    if 3 in chunks:
                        act.wait_ge(loaded_b, e * B_LOADS + 2 * B_LOADS)
                    act.wait_ge(s_init, INITS)
                    for c in chunks:
                        if c == 4 and not first_slot:
                            act.wait_ge(z_made, bits(act, word, AT_FIRST, S_BITS))
                        nc.scalar.copy(W[:, bass.ds(to + c * PIECE, PIECE)], raw[:, c * PIECE:(c + 1) * PIECE]).then_inc(split_hi[c // HALF], 1)

            def round_next(s, word):
                round_chunks(s, word, AT_A, (0, 1, 2))
                round_chunks(s, word, AT_B, (3, 4, 5))

            def weigh(s, s_plus_1):
                act.wait_ge(zb_ready, s_plus_1)
                nc.scalar.mul(zw[:], zb[:], share_of[:, bass.ds(s, 1)]).then_inc(zw_ready, 1)

            act.wait_ge(s_route, 1)
            copy_xT(1)
            sigmoid(1)
            act.wait_ge(lin_made, 1)
            copy_xT(2)
            act.wait_ge(s_meta, 1)
            word = word_of(act, 0)
            round_next(0, word)
            word = word_of(act, 1)
            copy_yT(1)
            sigmoid(2)
            act.wait_ge(lin_made, 2)
            copy_xT(3)
            round_next(1, word)
            weigh(0, 1)
            next_word = act.alloc_register("next_word")
            act.reg_load(next_word, meta[0:1, 2:3])
            with act.Fori(2, NS) as s:
                word = as_word(act, next_word)
                with act.If(bits(act, word, AT_END, 1)):
                    act.wait_ge(z_made, s - 1)
                    copy_yT(s)
                    act.reg_mov(next_word, 0)
                    act.wait_ge(scattered, s * 16 - 16)
                    weigh(s - 1, s)
                with act.If(bits(act, word, AT_LIVE, 1)):
                    act.wait_ge(z_made, s - 1)
                    copy_yT(s)
                    sigmoid(s + 1)
                    act.reg_load(next_word, meta[0:1, bass.ds(s + 1, 1)])
                    act.wait_ge(lin_made, s + 1)
                    copy_xT(s + 2)
                    round_next(s, word)
                    act.wait_ge(scattered, s * 16 - 16)
                    weigh(s - 1, s)

        @block.tensor
        def _(pe):
            pe.wait_ge(s_const, 1)
            pe.wait_ge(s_gws, 3)

            def turn(i):
                pe.wait_ge(s_x[i // TX], 16)
                if i >= NPS:
                    pe.wait_ge(s_lo, i - NPS + 1)
                for k in range(K):
                    last = nc.tensor.transpose(ps_turn[i % NPS][:, k * P:(k + 1) * P], x_sb[:, i, k * P:(k + 1) * P], ident[:])
                last.then_inc(s_turn, 1)

            def gate(g):
                pe.wait_ge(s_lo, (g + 1) * GROUP)
                if g >= 2:
                    pe.wait_ge(s_gated, g - 1)
                dst = ps_gated[g % 2]
                tiles = slice(g % 2 * GROUP, (g % 2 + 1) * GROUP)
                for k in range(K):
                    part = slice(k * P, (k + 1) * P)
                    nc.tensor.matmul(dst[0:2 * E, :], gw_split[:, k, :, :].rearrange("p a e -> p (a e)"),
                                     x_hi[:, tiles, part], start=(k == 0), stop=False)
                    last = nc.tensor.matmul(dst[0:E, :], gw_split[:, k, 0, :], x_lo[:, tiles, part],
                                            start=False, stop=(k == K - 1))
                last.then_inc(s_gx, 1)

            for i in range(NT + 2):
                if i < NT:
                    turn(i)
                if i > GROUP and i % GROUP == 1:
                    gate(i // GROUP - 1)
            def condition(i):
                if i >= 2:
                    pe.wait_ge(s_x0c, i - 1)
                nc.tensor.matmul(ps_x0[i % 2][:], w_diag[:, i, :], x_sb[:, i, :], start=True, stop=True).then_inc(s_x0, 1)

            pe.wait_ge(s_wd, 32)
            pe.wait_ge(s_gated, NT // GROUP - 1)
            condition(0)
            for i in range(NT):
                if i % GROUP == 0:
                    pe.wait_ge(s_gated, i // GROUP + 1)
                last = nc.tensor.transpose(ps_gate[:, i * 2 * E:(i + 1) * 2 * E], gated_x[:, i * P:(i + 1) * P], ident[0:2 * E, 0:2 * E])
            last.then_inc(s_back, 1)
            condition(1)
            pe.wait_ge(s_xg8, 1)
            for i in range(NT):
                if i % (NT // AMONG) == NT // AMONG // 2:
                    condition(EARLY + i // (NT // AMONG))
                last = nc.tensor.matmul(ps_log[:, i * E:(i + 1) * E], w_diag[:, i, :], xg8[:, i, :], start=True, stop=True)
            last.then_inc(s_log, 1)

            def ranks():
                pe.wait_ge(s_mask, 1)
                nc.tensor.matmul(ps_rank[:], before[:], mask[:].rearrange("p n e -> p (n e)"), start=True, stop=False)
                for j in range(NT):
                    last = nc.tensor.matmul(ps_rank[:, (j + 1) * E:].rearrange("p (n e) -> p n e", e=E), ones[:],
                                            mask[:, j:j + 1, :].to_broadcast([P, NT - j, E]), start=False, stop=(j == NT - 1))
                last.then_inc(s_rank, 1)

            def tabulate(c):
                pe.wait_ge(s_row_hot, c + 1)
                pe.wait_ge([s_hot, s_hot2][c], 1)
                for j in range(c * NT, (c + 1) * NT):
                    last = nc.tensor.matmul(ps_tab[:, 0:3 * NS], row_hot[:, j, :],
                                            slot_values[:, j, :, :].rearrange("p a s -> p (a s)"),
                                            start=(j == 0), stop=(j == NP - 1))
                return last

            for i in range(EARLY + AMONG, NT):
                if i == RANK_AT:
                    ranks()
                condition(i)
            tabulate(0)
            tabulate(1).then_inc(s_tab, 1)

            def turn_x(rows16):
                pe.wait_ge(gathered, rows16)
                for k in range(K):
                    last = nc.tensor.transpose(ps_xT[:, k * P:(k + 1) * P], xg[:, k * P:(k + 1) * P], ident[:])
                last.then_inc(xT_made, 1)

            def turn_y(s_plus_1):
                pe.wait_ge(y_ready, s_plus_1)
                for k in range(K):
                    last = nc.tensor.transpose(ps_yT[:, k * P:(k + 1) * P], y[:, k * P:(k + 1) * P], ident[:])
                last.then_inc(yT_made, 1)

            def product(dst, hi, lo, w_at, at, done):
                for k in range(K):
                    part = slice(k * P, (k + 1) * P)
                    w_hi = W[:, bass.ds(w_at + (at + k * I), I)]
                    w_lo = W[:, bass.ds(w_at + (WLEN + at + k * I), I)]
                    nc.tensor.matmul(dst[:], hi[:, part], w_hi, start=(k == 0), stop=False)
                    nc.tensor.matmul(dst[:], hi[:, part], w_lo, start=False, stop=False)
                    last = nc.tensor.matmul(dst[:], lo[:, part], w_hi, start=False, stop=(k == K - 1))
                last.then_inc(done, 1)

            def glu_ready(e):
                pe.wait_ge(split_dve, e * 4 + (DVE_START - 2))

            def lin_ready(e):
                pe.wait_ge(split_dve, e * 4 + DVE_START)

            def down_ready(e):
                pe.wait_ge(split_pool, e * 2 + 2)

            turn_x(16)
            pe.wait_ge(split_pool, 2)
            w_at = 0
            pe.wait_ge(xT_ready, 1)
            product(ps_glu, xT_hi, xT_lo, w_at, GLU, glu_made)
            product(ps_lin, xT_hi, xT_lo, w_at, LIN, lin_made)
            turn_x(32)
            pe.wait_ge(s_meta, 1)
            e = expert(pe, word_of(pe, 1))
            w_at, last_at = place_of_w(pe, e), 0
            glu_ready(e)
            pe.wait_ge(xT_ready, 2)
            pe.wait_ge(g_ready, 1)
            product(ps_glu, xT_hi, xT_lo, w_at, GLU, glu_made)
            turn_y(1)
            lin_ready(e)
            product(ps_lin, xT_hi, xT_lo, w_at, LIN, lin_made)
            turn_x(48)
            pe.wait_ge(yT_ready, 1)
            product(ps_z, yT_hi, yT_lo, last_at, DOWN, z_made)
            next_word = pe.alloc_register("next_word")
            pe.reg_load(next_word, meta[0:1, 2:3])
            with pe.Fori(2, NS) as s:
                word = as_word(pe, next_word)
                with pe.If(bits(pe, word, AT_LIVE, 1)):
                    e, before_e = expert(pe, word), expert_before(pe, word)
                    w_at, last_at = place_of_w(pe, e), place_of_w(pe, before_e)
                    glu_ready(e)
                    pe.wait_ge(xT_ready, s + 1)
                    pe.wait_ge(g_ready, s)
                    product(ps_glu, xT_hi, xT_lo, w_at, GLU, glu_made)
                    turn_y(s)
                    lin_ready(e)
                    product(ps_lin, xT_hi, xT_lo, w_at, LIN, lin_made)
                    turn_x(s * 16 + 32)
                    pe.reg_load(next_word, meta[0:1, bass.ds(s + 1, 1)])
                    down_ready(before_e)
                    pe.wait_ge(yT_ready, s)
                    pe.wait_ge(zb_ready, s - 1)
                    product(ps_z, yT_hi, yT_lo, last_at, DOWN, z_made)
                with pe.If(bits(pe, word, AT_END, 1)):
                    before_e = expert_before(pe, word)
                    last_at = place_of_w(pe, before_e)
                    turn_y(s)
                    pe.reg_mov(next_word, 0)
                    down_ready(before_e)
                    pe.wait_ge(yT_ready, s)
                    pe.wait_ge(zb_ready, s - 1)
                    product(ps_z, yT_hi, yT_lo, last_at, DOWN, z_made)

        @block.vector
        def _(dve):
            v = nc.vector
            chain = [0]

            def link(ins):
                chain[0] += 1
                ins.then_inc(s_dve, 1)
                dve.wait_ge(s_dve, chain[0])

            dve.wait_ge(s_gate, 32)
            v.tensor_copy(gw_split[:, :, 0, :], gw[:]).then_inc(s_gws, 1)
            dve.wait_ge(s_gws, 1)
            v.tensor_tensor(gw_split[:, :, 1, :], gw[:], gw_split[:, :, 0, :].bitcast(F32), ALU.subtract).then_inc(s_gws, 1)
            link(v.memset(mask[:, NT, :], 0.0))
            v.memset(tiles_of[:], 0.0).then_inc(s_gws, 1)
            for i in range(NT):
                dve.wait_ge(s_hi, i + 1)
                if i >= NXT:
                    dve.wait_ge(s_gx, (i - NXT) // GROUP + 1)
                v.tensor_tensor(x_lo[:, i % NXT, :], ps_turn[i % NPS][:], x_hi[:, i % NXT, :].bitcast(F32),
                                ALU.subtract).then_inc(s_lo, 1)
            dve.wait_ge(s_back, 1)
            link(v.tensor_copy(gated[:].rearrange("p n a e -> p (n a e)"), ps_gate[:, 0:NT * 2 * E]))
            v.tensor_tensor(xg8[:], gated[:, :, 0, :], gated[:, :, 1, :], ALU.add).then_inc(s_xg8, 1)

            dve.wait_ge(s_log, 1)
            dve.wait_ge(s_const, N_CONST - 3)
            te = [P, NT, E]
            link(v.tensor_tensor(logits[:], ps_log[:].rearrange("p (n e) -> p n e", e=E),
                                 gb[:].unsqueeze(1).to_broadcast(te), ALU.add))
            rev = rev_id[:].unsqueeze(1).to_broadcast(te)
            src = logits
            for c in range(2):
                link(v.tensor_reduce(best[:, c, :], src[:], AX_X, ALU.max))
                link(v.tensor_tensor(hit[:], src[:], best[:, c, :].unsqueeze(2).to_broadcast(te), ALU.is_equal))
                link(v.tensor_tensor(key[:], hit[:], rev, ALU.mult))
                link(v.tensor_reduce(pick[:, c, :], key[:], AX_X, ALU.max))
                link(v.tensor_tensor(chosen[:, c, :, :], rev, pick[:, c, :].unsqueeze(2).to_broadcast(te), ALU.is_equal))
                if c == 0:
                    link(v.scalar_tensor_tensor(out=rest[:], in0=chosen[:, 0, :, :], scalar=FLOOR, in1=logits[:],
                                                op0=ALU.mult, op1=ALU.add))
                    src = rest
            v.tensor_tensor(mask[:, 0:NT, :], chosen[:, 0, :, :], chosen[:, 1, :, :], ALU.add).then_inc(s_mask, 1)
            v.tensor_tensor(gap[:], best[:, 1, :], best[:, 0, :], ALU.subtract).then_inc(s_gap, 1)
            dve.wait_ge(s_egap, 1)
            link(v.tensor_scalar(den[:], egap[:], 1.0, None, ALU.add))
            link(v.reciprocal(share[:, 0:NT], den[:]))
            link(v.tensor_tensor(share[:, NT:NP], share[:, 0:NT], egap[:], ALU.mult))
            link(v.tensor_copy(share_hi[:], share[:]))
            link(v.tensor_copy(values[:, :, 1], share_hi[:].bitcast(F32)))
            link(v.tensor_tensor(values[:, :, 2], share[:], share_hi[:].bitcast(F32), ALU.subtract))
            dve.wait_ge(s_rank, 1)
            een = [P, E, NT]
            link(v.tensor_tensor(full[:], ps_rank[:, NT * E:].unsqueeze(2).to_broadcast(een),
                                 fill_id[:].unsqueeze(1).to_broadcast(een), ALU.is_gt))
            link(v.tensor_reduce(tiles_of[:], full[:], AX_X, ALU.add))
            link(v.tensor_scalar(tiles_of[:], tiles_of[:], 1.0, None, ALU.max))
            link(v.tensor_tensor(bef[:], earlier[:], tiles_of[:].unsqueeze(1).to_broadcast([P, E, E]), ALU.mult))
            link(v.tensor_reduce(base[:], bef[:], AX_X, ALU.add))
            link(v.tensor_scalar(base_rows[:], base[:], float(P), None, ALU.mult))
            link(v.tensor_tensor(place_e[:], ps_rank[:, 0:NT * E].rearrange("p (n e) -> p n e", e=E),
                                 base_rows[:].unsqueeze(1).to_broadcast(te), ALU.add))
            link(v.tensor_tensor(place_k[:], chosen[:], place_e[:].unsqueeze(1).to_broadcast([P, 2, NT, E]), ALU.mult))
            link(v.tensor_reduce(place[:], place_k[:].rearrange("p c n e -> p (c n) e"), AX_X, ALU.add))
            link(v.tensor_copy(place_i[:], place[:]))
            link(v.tensor_scalar(row_of[:], place_i[:], P - 1, None, ALU.bitwise_and))
            link(v.tensor_scalar(slot_of[:], place_i[:], P.bit_length() - 1, None, ALU.arith_shift_right))
            v.tensor_tensor(slot_hot[:], slot_of[:].unsqueeze(2).to_broadcast([P, NP, NS]),
                            slot_id[:].unsqueeze(1).to_broadcast([P, NP, NS]), ALU.is_equal).then_inc(s_slot_hot, 1)
            dve.wait_ge(s_slot_hot, 1)
            spread_values(v, 0).then_inc(s_hot, 1)
            dve.wait_ge(s_wr, 16)
            for c in range(2):
                h = slice(c * NT, (c + 1) * NT)
                v.tensor_tensor(row_hot[:, h, :], row_of[:, h].unsqueeze(2).to_broadcast([P, NT, P]),
                                row_id[:].unsqueeze(1).to_broadcast([P, NT, P]), ALU.is_equal).then_inc(s_row_hot, 1)
            ese = [1, NS, E]
            link(v.tensor_tensor(ends[:], base[0:1, :], tiles_of[0:1, :], ALU.add))
            link(v.tensor_tensor(over[:], slot_id[0:1, :].unsqueeze(2).to_broadcast(ese),
                                 ends[:].unsqueeze(1).to_broadcast(ese), ALU.is_ge))
            link(v.tensor_reduce(ended[:], over[:], AX_X, ALU.add))
            link(v.tensor_scalar(expert_of[:], ended[:], float(E - 1), None, ALU.min))
            v.tensor_scalar(live[:], ended[:], float(E), None, ALU.is_lt)
            v.tensor_scalar(at_end[:], slot_id[0:1, :], ends[:, E - 1:E], float(1 << AT_END), ALU.is_equal, ALU.mult)
            v.memset(meta[:, NS:NS + 1], 0)
            dve.wait_ge(s_tab, 1)
            link(v.tensor_copy(table[:].rearrange("p a s -> p (a s)"), ps_tab[:, 0:3 * NS]))
            link(v.tensor_scalar(fill[:], table[:, 0, :], 0.0, pad_id[:, 0:1], ALU.is_equal, ALU.mult))
            v.tensor_tensor(share_of[:], table[:, 1, :], table[:, 2, :], ALU.add)
            v.scalar_tensor_tensor(out=tokens[:], in0=table[:, 0, :], scalar=-1.0, in1=fill[:],
                                   op0=ALU.add, op1=ALU.add).then_inc(s_route, 1)


            link(v.tensor_tensor(over[:], over[:], ends[:].unsqueeze(1).to_broadcast(ese), ALU.mult))
            link(v.tensor_reduce(first_of[:], over[:], AX_X, ALU.max))
            link(v.tensor_scalar(first_of[:], first_of[:], 1.0, None, ALU.max))
            link(v.scalar_tensor_tensor(out=packed[:], in0=live[:], scalar=float(1 << AT_LIVE), in1=expert_of[:],
                                        op0=ALU.mult, op1=ALU.add))
            link(v.tensor_tensor(packed[:], packed[:], at_end[:], ALU.add))
            link(v.scalar_tensor_tensor(out=packed[:], in0=first_of[:], scalar=float(1 << AT_FIRST), in1=packed[:],
                                        op0=ALU.mult, op1=ALU.add))
            link(v.scalar_tensor_tensor(out=packed[:, 1:], in0=expert_of[:, 0:NS - 1], scalar=float(1 << AT_BEFORE),
                                        in1=packed[:, 1:], op0=ALU.mult, op1=ALU.add))
            link(v.tensor_scalar(lasts[:], ends[:], -1.0, None, ALU.add))
            link(v.tensor_scalar(turn_a[:], ends[:], -2.0, None, ALU.add))
            link(v.tensor_tensor(turn_a[:], turn_a[:], base[0:1, :], ALU.max))
            link(v.tensor_scalar(turn_b[:], base[0:1, :], 1.0, None, ALU.add))
            link(v.tensor_tensor(turn_a[:], turn_a[:], turn_b[:], ALU.min))
            link(v.tensor_scalar(turn_b[:], base[0:1, :], 2.0, None, ALU.add))
            link(v.tensor_tensor(turn_b[:], turn_b[:], lasts[:], ALU.min))
            esf = [1, NS, E - 1]
            for half, turn_of, at in ((0, turn_a, AT_A), (1, turn_b, AT_B)):
                link(v.tensor_tensor(at_turn[:], slot_id[0:1, :].unsqueeze(2).to_broadcast(esf),
                                     turn_of[:, 0:E - 1].unsqueeze(1).to_broadcast(esf), ALU.is_equal))
                link(v.tensor_reduce(splits[:, half, :], at_turn[:], AX_X, ALU.max))
                link(v.scalar_tensor_tensor(out=[packed[:], meta[:, 0:NS]][half], in0=splits[:, half, :], scalar=float(1 << at),
                                            in1=packed[:], op0=ALU.mult, op1=ALU.add))
            v.memset(turn_a[:], 0.0).then_inc(s_meta, 1)
            v.memset(turn_b[:], 0.0).then_inc(split_dve, DVE_START)

            def glu(b_at, s_plus_1):
                dve.wait_ge(glu_made, s_plus_1)
                v.tensor_tensor(g[:], ps_glu[:], BI[:, bass.ds(b_at + BG, I)], ALU.add).then_inc(g_ready, 1)

            def linear(b_at, s_plus_1):
                dve.wait_ge(lin_made, s_plus_1)
                v.tensor_tensor(lin[:], ps_lin[:], BI[:, bass.ds(b_at + BL, I)], ALU.add).then_inc(part_ready, 1)

            def gate_g(s_plus_1):
                dve.wait_ge(sig_ready, s_plus_1)
                v.tensor_tensor(gs[:], g[:], sig[:], ALU.mult).then_inc(part_ready, 1)

            def join(parts):
                dve.wait_ge(part_ready, parts)
                v.scalar_tensor_tensor(out=y[:], in0=lin[:], scalar=1.0, in1=gs[:],
                                       op0=ALU.add, op1=ALU.mult).then_inc(y_ready, 1)

            def low_xT(s_plus_1):
                dve.wait_ge(xT_rounded, s_plus_1)
                v.tensor_tensor(xT_lo[:], ps_xT[:], xT_hi[:].bitcast(F32), ALU.subtract).then_inc(xT_ready, 1)

            def low_yT(s_plus_1):
                dve.wait_ge(yT_rounded, s_plus_1)
                v.tensor_tensor(yT_lo[:], ps_yT[:], yT_hi[:].bitcast(F32), ALU.subtract).then_inc(yT_ready, 1)

            def down(b_at, s_plus_1):
                dve.wait_ge(z_made, s_plus_1)
                v.tensor_tensor(zb[:], ps_z[:], BI[:, bass.ds(b_at + BD, H)], ALU.add).then_inc(zb_ready, 1)

            def low_chunks(word, flag, chunks):
                with dve.If(bits(dve, word, flag, 1)):
                    e = expert(dve, word)
                    to = next_place_of_w(dve, e)
                    for c in chunks:
                        dve.wait_ge(split_hi[c // HALF], e * HALF + (HALF + c % HALF + 1))
                        v.tensor_tensor(W[:, bass.ds(to + (WLEN + c * PIECE), PIECE)], raw[:, c * PIECE:(c + 1) * PIECE],
                                        W[:, bass.ds(to + c * PIECE, PIECE)].bitcast(F32), ALU.subtract).then_inc(split_dve, 1)

            low_xT(1)
            dve.wait_ge(s_meta, 1)
            word = word_of(dve, 0)
            b_at = 0
            glu(b_at, 1)
            linear(b_at, 1)
            low_xT(2)
            gate_g(1)
            join(2)
            low_chunks(word, AT_A, (0, 1))
            low_chunks(word, AT_B, (2, 3))
            word = word_of(dve, 1)
            b_at, last_at = place_of_b(dve, expert(dve, word)), 0
            glu(b_at, 2)
            low_yT(1)
            linear(b_at, 2)
            low_xT(3)
            gate_g(2)
            join(4)
            down(last_at, 1)
            low_chunks(word, AT_A, (0, 1))
            low_chunks(word, AT_B, (2, 3))
            next_word = dve.alloc_register("next_word")
            dve.reg_load(next_word, meta[0:1, 2:3])
            with dve.Fori(2, NS) as s:
                word = as_word(dve, next_word)
                with dve.If(bits(dve, word, AT_END, 1)):
                    last_at = place_of_b(dve, expert_before(dve, word))
                    low_yT(s)
                    dve.reg_mov(next_word, 0)
                    dve.wait_ge(zw_ready, s - 1)
                    down(last_at, s)
                with dve.If(bits(dve, word, AT_LIVE, 1)):
                    b_at = place_of_b(dve, expert(dve, word))
                    last_at = place_of_b(dve, expert_before(dve, word))
                    glu(b_at, s + 1)
                    low_yT(s)
                    linear(b_at, s + 1)
                    low_xT(s + 2)
                    gate_g(s + 1)
                    dve.reg_load(next_word, meta[0:1, bass.ds(s + 1, 1)])
                    join(s * 2 + 2)
                    dve.wait_ge(zw_ready, s - 1)
                    down(last_at, s)
                    low_chunks(word, AT_A, (0, 1))
                    low_chunks(word, AT_B, (2, 3))


def kernel(x, itok_B_1_198, L0_cond_weights, L0_ffn_gate_w, L0_ffn_gate_b, L0_ffn_w1, L0_ffn_b1, L0_ffn_w2, L0_ffn_b2):
    import numpy as np
    import concourse.bacc as bacc
    from concourse.bass_utils import run_bass_kernel_spmd

    B, C, H = x.shape
    E = L0_ffn_w1.shape[0]
    K = H // P

    def by_rows(w):
        w = np.asarray(w)
        return w.transpose(0, 2, 1).reshape(E, K, P, w.shape[1]).transpose(0, 2, 1, 3).reshape(E, P, K * w.shape[1])

    w1, b1 = np.asarray(L0_ffn_w1), np.asarray(L0_ffn_b1)
    arrays = {
        "x": np.asarray(x).reshape(B * C, H),
        "cond": np.asarray(itok_B_1_198).reshape(B, 1),
        "cond_w": np.asarray(L0_cond_weights),
        "gate_w": np.asarray(L0_ffn_gate_w).T.reshape(K, P, E).transpose(1, 0, 2),
        "gate_b": np.asarray(L0_ffn_gate_b),
        "ffn_w": np.concatenate([by_rows(w1[:, 0::2]), by_rows(w1[:, 1::2]), by_rows(L0_ffn_w2)], axis=2),
        "ffn_b": np.concatenate([b1[:, 0::2], b1[:, 1::2], np.asarray(L0_ffn_b2)], axis=1),
    }
    arrays = {k: np.ascontiguousarray(a) for k, a in arrays.items()}
    nc = bacc.Bacc("TRN2", target_bir_lowering=False, num_devices=1)
    ins = [nc.dram_tensor(n, a.shape, mybir.dt.from_np(a.dtype), kind="ExternalInput").ap() for n, a in arrays.items()]
    cond_rows = nc.dram_tensor("cond_rows", (B, C * C), F32, kind="Internal").ap()
    x0_rows = nc.dram_tensor("x0_rows", (B * C + P, H), F32, kind="Internal").ap()
    out = nc.dram_tensor("out", (B * C + P, H), F32, kind="ExternalOutput").ap()
    adaln_moe_kernel(nc, *ins, cond_rows, x0_rows, out)
    r = run_bass_kernel_spmd(nc, [arrays], core_ids=[0])
    return r.results[0]["out"][:B * C].reshape(B, C, H)
```
